# Optimizing a Trainium2 kernel written in Bass

```python
import numpy as np
import jax
import jax.numpy as jnp

def _softmax(x, axis=-1):
    return jax.nn.softmax(x, axis=axis)
def _gelu(x):
    return jax.nn.gelu(x, approximate=True)
def _silu(x):
    return jax.nn.silu(x)
def _sigmoid(x):
    return jax.nn.sigmoid(x)
def _layernorm(x, axis=-1, eps=1e-5):
    m = jnp.mean(x, axis=axis, keepdims=True)
    v = jnp.var(x, axis=axis, keepdims=True)
    return (x - m) / jnp.sqrt(v + eps)
def _scatter_add(tgt, idx, src, axis=0):
    return tgt.at[idx].add(src)
def _segment_sum(src, seg, n):
    return jax.ops.segment_sum(src, seg, n)

kernel_name = 'mk_conv_preact_d4_conv_nhwc64_99d737'

def setup_inputs(seed: int = 0):
    np.random.seed(seed)
    _w = jnp.asarray
    def _rec_inputs():
        import jax
        import jax.numpy as jnp
        _gk = jax.random.key(seed)
        x = -0.0005207 + 1.001 * jax.random.normal(jax.random.fold_in(_gk, 1), (4, 128, 64, 64), jnp.float32)
        return x
    x = _rec_inputs()
    def _L0_conv_setup():
        import jax, jax.numpy as jnp
        import numpy as np
        D_MODEL = 64
        D_INNER = 2 * D_MODEL
        D_STATE = 16
        D_CONV = 4
        DT_RANK = (D_MODEL + 15) // 16
        B, T, N, F = (4, 128, 64, 64)

        def _mamba(seq, W_in, conv_w, conv_b, W_x, W_dt, b_dt, A_log, Dp, W_out):
            Beff, L, _ = seq.shape
            xz = seq @ W_in.T
            u, z = jnp.split(xz, 2, axis=-1)
            u_pad = jnp.pad(u, ((0, 0), (D_CONV - 1, 0), (0, 0)))
            u = sum((u_pad[:, k:k + L, :] * conv_w[:, k] for k in range(D_CONV))) + conv_b
            u = jax.nn.silu(u)
            x_dbl = u @ W_x.T
            dt = jax.nn.softplus(x_dbl[..., :DT_RANK] @ W_dt.T + b_dt)
            Bmat = x_dbl[..., DT_RANK:DT_RANK + D_STATE]
            Cmat = x_dbl[..., DT_RANK + D_STATE:]
            A = -jnp.exp(A_log)

            def step(h, inp):
                u_t, dt_t, B_t, C_t = inp
                h = jnp.exp(dt_t[:, :, None] * A) * h + (dt_t * u_t)[:, :, None] * B_t[:, None, :]
                y = jnp.einsum('bds,bs->bd', h, C_t)
                return (h, y)
            h0 = jnp.zeros((Beff, D_INNER, D_STATE), seq.dtype)
            xs = (u.transpose(1, 0, 2), dt.transpose(1, 0, 2), Bmat.transpose(1, 0, 2), Cmat.transpose(1, 0, 2))
            _, ys = jax.lax.scan(step, h0, xs)
            y = ys.transpose(1, 0, 2) + u * Dp
            y = y * jax.nn.silu(z)
            return y @ W_out.T
        key = jax.random.key(seed)
        ks = jax.random.split(key, 8)
        s = 0.02
        x = jax.random.normal(ks[0], (B, T, N, F), jnp.float32)
        W_in = jax.random.normal(ks[1], (2 * D_INNER, D_MODEL), jnp.float32) * s
        conv_w = jax.random.normal(ks[2], (D_INNER, D_CONV), jnp.float32) * s
        conv_b = jnp.zeros((D_INNER,), jnp.float32)
        W_x = jax.random.normal(ks[3], (DT_RANK + 2 * D_STATE, D_INNER), jnp.float32) * s
        W_dt = jax.random.normal(ks[4], (D_INNER, DT_RANK), jnp.float32) * s
        b_dt = jax.random.normal(ks[5], (D_INNER,), jnp.float32) * 0.1 - 4.0
        A_log = jnp.log(jnp.broadcast_to(jnp.arange(1, D_STATE + 1, dtype=jnp.float32), (D_INNER, D_STATE)))
        Dp = jnp.ones((D_INNER,), jnp.float32)
        W_out = jax.random.normal(ks[6], (D_MODEL, D_INNER), jnp.float32) * s
        return dict(x=x, W_in=W_in, conv_w=conv_w, conv_b=conv_b, W_x=W_x, W_dt=W_dt, b_dt=b_dt, A_log=A_log, Dp=Dp, W_out=W_out)
    _L0_conv_all = _L0_conv_setup()
    _L0_conv_in = {k: v for k, v in _L0_conv_all.items() if k in ('W_in', 'conv_w', 'conv_b', 'W_x', 'W_dt', 'b_dt', 'A_log', 'Dp', 'W_out', )}
    del _L0_conv_all

    def _L1_conv_setup():
        import jax, jax.numpy as jnp
        import numpy as np
        D_MODEL = 64
        D_INNER = 2 * D_MODEL
        D_STATE = 16
        D_CONV = 4
        DT_RANK = (D_MODEL + 15) // 16
        B, T, N, F = (4, 128, 64, 64)

        def _mamba(seq, W_in, conv_w, conv_b, W_x, W_dt, b_dt, A_log, Dp, W_out):
            Beff, L, _ = seq.shape
            xz = seq @ W_in.T
            u, z = jnp.split(xz, 2, axis=-1)
            u_pad = jnp.pad(u, ((0, 0), (D_CONV - 1, 0), (0, 0)))
            u = sum((u_pad[:, k:k + L, :] * conv_w[:, k] for k in range(D_CONV))) + conv_b
            u = jax.nn.silu(u)
            x_dbl = u @ W_x.T
            dt = jax.nn.softplus(x_dbl[..., :DT_RANK] @ W_dt.T + b_dt)
            Bmat = x_dbl[..., DT_RANK:DT_RANK + D_STATE]
            Cmat = x_dbl[..., DT_RANK + D_STATE:]
            A = -jnp.exp(A_log)

            def step(h, inp):
                u_t, dt_t, B_t, C_t = inp
                h = jnp.exp(dt_t[:, :, None] * A) * h + (dt_t * u_t)[:, :, None] * B_t[:, None, :]
                y = jnp.einsum('bds,bs->bd', h, C_t)
                return (h, y)
            h0 = jnp.zeros((Beff, D_INNER, D_STATE), seq.dtype)
            xs = (u.transpose(1, 0, 2), dt.transpose(1, 0, 2), Bmat.transpose(1, 0, 2), Cmat.transpose(1, 0, 2))
            _, ys = jax.lax.scan(step, h0, xs)
            y = ys.transpose(1, 0, 2) + u * Dp
            y = y * jax.nn.silu(z)
            return y @ W_out.T
        key = jax.random.key(seed)
        ks = jax.random.split(key, 8)
        s = 0.02
        x = jax.random.normal(ks[0], (B, T, N, F), jnp.float32)
        W_in = jax.random.normal(ks[1], (2 * D_INNER, D_MODEL), jnp.float32) * s
        conv_w = jax.random.normal(ks[2], (D_INNER, D_CONV), jnp.float32) * s
        conv_b = jnp.zeros((D_INNER,), jnp.float32)
        W_x = jax.random.normal(ks[3], (DT_RANK + 2 * D_STATE, D_INNER), jnp.float32) * s
        W_dt = jax.random.normal(ks[4], (D_INNER, DT_RANK), jnp.float32) * s
        b_dt = jax.random.normal(ks[5], (D_INNER,), jnp.float32) * 0.1 - 4.0
        A_log = jnp.log(jnp.broadcast_to(jnp.arange(1, D_STATE + 1, dtype=jnp.float32), (D_INNER, D_STATE)))
        Dp = jnp.ones((D_INNER,), jnp.float32)
        W_out = jax.random.normal(ks[6], (D_MODEL, D_INNER), jnp.float32) * s
        return dict(x=x, W_in=W_in, conv_w=conv_w, conv_b=conv_b, W_x=W_x, W_dt=W_dt, b_dt=b_dt, A_log=A_log, Dp=Dp, W_out=W_out)
    _L1_conv_all = _L1_conv_setup()
    _L1_conv_in = {k: v for k, v in _L1_conv_all.items() if k in ('W_in', 'conv_w', 'conv_b', 'W_x', 'W_dt', 'b_dt', 'A_log', 'Dp', 'W_out', )}
    del _L1_conv_all

    def _L2_conv_setup():
        import jax, jax.numpy as jnp
        import numpy as np
        N = 64
        CH = 128
        RES = 64
        LRF = 4
        LH = RES // LRF
        LW = RES // LRF
        L = LH * LW
        K = max(1, int(L * 0.1))
        NB = LRF * LRF
        OC = CH // 10 + 1
        INDIM = K * CH + L
        HID = INDIM
        OUTDIM = L * OC
        key = jax.random.key(seed)
        ks = jax.random.split(key, 8)
        x = jax.random.normal(ks[0], (N, CH, RES, RES), jnp.float32)
        conv_w = jax.random.normal(ks[1], (NB, CH), jnp.float32) * 0.05
        W1 = jax.random.normal(ks[2], (INDIM, HID), jnp.float32) * 0.02
        b1 = jnp.zeros((HID,), jnp.float32)
        W2 = jax.random.normal(ks[3], (HID, OUTDIM), jnp.float32) * 0.02
        b2 = jnp.zeros((OUTDIM,), jnp.float32)
        out_w = jax.random.normal(ks[4], (CH, OC), jnp.float32) * 0.05
        return dict(x=x, conv_w=conv_w, W1=W1, b1=b1, W2=W2, b2=b2, out_w=out_w, tau=1)
    _L2_conv_all = _L2_conv_setup()
    _L2_conv_in = {k: v for k, v in _L2_conv_all.items() if k in ('conv_w', 'W1', 'b1', 'W2', 'b2', 'out_w', )}
    del _L2_conv_all

    def _L3_conv_setup():
        import jax, jax.numpy as jnp
        import numpy as np

        def _avg_pool(x, s):
            if s == 1:
                return x
            B, C, H, W = x.shape
            return x.reshape(B, C, H // s, s, W // s, s).mean(axis=(3, 5))

        def _attention(x):
            B, C, H, W = x.shape
            xf = x.reshape(B, C, H * W)
            scores = jnp.einsum('bcn,bcm->bnm', xf, xf)
            attn = jax.nn.softmax(scores, axis=-1)
            out = jnp.einsum('bnm,bcm->bcn', attn, xf)
            return out.reshape(B, C, H, W)
        key = jax.random.key(seed)
        x = jax.random.normal(key, (4, 128, 64, 64), dtype=jnp.float32)
        return {'x': x}
    _L3_conv_all = _L3_conv_setup()
    _L3_conv_in = {k: v for k, v in _L3_conv_all.items() if k in ()}
    del _L3_conv_all

    return {
        "x": x,
        "L0_conv_W_in": _L0_conv_in["W_in"],
        "L0_conv_conv_w": _L0_conv_in["conv_w"],
        "L0_conv_conv_b": _L0_conv_in["conv_b"],
        "L0_conv_W_x": _L0_conv_in["W_x"],
        "L0_conv_W_dt": _L0_conv_in["W_dt"],
        "L0_conv_b_dt": _L0_conv_in["b_dt"],
        "L0_conv_A_log": _L0_conv_in["A_log"],
        "L0_conv_Dp": _L0_conv_in["Dp"],
        "L0_conv_W_out": _L0_conv_in["W_out"],
        "L1_conv_W_in": _L1_conv_in["W_in"],
        "L1_conv_conv_w": _L1_conv_in["conv_w"],
        "L1_conv_conv_b": _L1_conv_in["conv_b"],
        "L1_conv_W_x": _L1_conv_in["W_x"],
        "L1_conv_W_dt": _L1_conv_in["W_dt"],
        "L1_conv_b_dt": _L1_conv_in["b_dt"],
        "L1_conv_A_log": _L1_conv_in["A_log"],
        "L1_conv_Dp": _L1_conv_in["Dp"],
        "L1_conv_W_out": _L1_conv_in["W_out"],
        "L2_conv_conv_w": _L2_conv_in["conv_w"],
        "L2_conv_W1": _L2_conv_in["W1"],
        "L2_conv_b1": _L2_conv_in["b1"],
        "L2_conv_W2": _L2_conv_in["W2"],
        "L2_conv_b2": _L2_conv_in["b2"],
        "L2_conv_out_w": _L2_conv_in["out_w"],
    }

def reference(x, L0_conv_W_in, L0_conv_conv_w, L0_conv_conv_b, L0_conv_W_x, L0_conv_W_dt, L0_conv_b_dt, L0_conv_A_log, L0_conv_Dp, L0_conv_W_out, L1_conv_W_in, L1_conv_conv_w, L1_conv_conv_b, L1_conv_W_x, L1_conv_W_dt, L1_conv_b_dt, L1_conv_A_log, L1_conv_Dp, L1_conv_W_out, L2_conv_conv_w, L2_conv_W1, L2_conv_b1, L2_conv_W2, L2_conv_b2, L2_conv_out_w):
    import jax
    import jax.numpy as jnp
    def _L0_conv_ref(x, W_in, conv_w, conv_b, W_x, W_dt, b_dt, A_log, Dp, W_out):
        import jax, jax.numpy as jnp
        import numpy as np
        D_MODEL = 64
        D_INNER = 2 * D_MODEL
        D_STATE = 16
        D_CONV = 4
        DT_RANK = (D_MODEL + 15) // 16
        B, T, N, F = (4, 128, 64, 64)

        def _mamba(seq, W_in, conv_w, conv_b, W_x, W_dt, b_dt, A_log, Dp, W_out):
            Beff, L, _ = seq.shape
            xz = seq @ W_in.T
            u, z = jnp.split(xz, 2, axis=-1)
            u_pad = jnp.pad(u, ((0, 0), (D_CONV - 1, 0), (0, 0)))
            u = sum((u_pad[:, k:k + L, :] * conv_w[:, k] for k in range(D_CONV))) + conv_b
            u = jax.nn.silu(u)
            x_dbl = u @ W_x.T
            dt = jax.nn.softplus(x_dbl[..., :DT_RANK] @ W_dt.T + b_dt)
            Bmat = x_dbl[..., DT_RANK:DT_RANK + D_STATE]
            Cmat = x_dbl[..., DT_RANK + D_STATE:]
            A = -jnp.exp(A_log)

            def step(h, inp):
                u_t, dt_t, B_t, C_t = inp
                h = jnp.exp(dt_t[:, :, None] * A) * h + (dt_t * u_t)[:, :, None] * B_t[:, None, :]
                y = jnp.einsum('bds,bs->bd', h, C_t)
                return (h, y)
            h0 = jnp.zeros((Beff, D_INNER, D_STATE), seq.dtype)
            xs = (u.transpose(1, 0, 2), dt.transpose(1, 0, 2), Bmat.transpose(1, 0, 2), Cmat.transpose(1, 0, 2))
            _, ys = jax.lax.scan(step, h0, xs)
            y = ys.transpose(1, 0, 2) + u * Dp
            y = y * jax.nn.silu(z)
            return y @ W_out.T
        b, t, n, f = x.shape
        seq = x.transpose(0, 2, 1, 3).reshape(b * n, t, f)
        out = _mamba(seq, W_in, conv_w, conv_b, W_x, W_dt, b_dt, A_log, Dp, W_out)
        return out.reshape(b, n, t, f).transpose(0, 2, 1, 3)

    def _L1_conv_ref(x, W_in, conv_w, conv_b, W_x, W_dt, b_dt, A_log, Dp, W_out):
        import jax, jax.numpy as jnp
        import numpy as np
        D_MODEL = 64
        D_INNER = 2 * D_MODEL
        D_STATE = 16
        D_CONV = 4
        DT_RANK = (D_MODEL + 15) // 16
        B, T, N, F = (4, 128, 64, 64)

        def _mamba(seq, W_in, conv_w, conv_b, W_x, W_dt, b_dt, A_log, Dp, W_out):
            Beff, L, _ = seq.shape
            xz = seq @ W_in.T
            u, z = jnp.split(xz, 2, axis=-1)
            u_pad = jnp.pad(u, ((0, 0), (D_CONV - 1, 0), (0, 0)))
            u = sum((u_pad[:, k:k + L, :] * conv_w[:, k] for k in range(D_CONV))) + conv_b
            u = jax.nn.silu(u)
            x_dbl = u @ W_x.T
            dt = jax.nn.softplus(x_dbl[..., :DT_RANK] @ W_dt.T + b_dt)
            Bmat = x_dbl[..., DT_RANK:DT_RANK + D_STATE]
            Cmat = x_dbl[..., DT_RANK + D_STATE:]
            A = -jnp.exp(A_log)

            def step(h, inp):
                u_t, dt_t, B_t, C_t = inp
                h = jnp.exp(dt_t[:, :, None] * A) * h + (dt_t * u_t)[:, :, None] * B_t[:, None, :]
                y = jnp.einsum('bds,bs->bd', h, C_t)
                return (h, y)
            h0 = jnp.zeros((Beff, D_INNER, D_STATE), seq.dtype)
            xs = (u.transpose(1, 0, 2), dt.transpose(1, 0, 2), Bmat.transpose(1, 0, 2), Cmat.transpose(1, 0, 2))
            _, ys = jax.lax.scan(step, h0, xs)
            y = ys.transpose(1, 0, 2) + u * Dp
            y = y * jax.nn.silu(z)
            return y @ W_out.T
        b, t, n, f = x.shape
        seq = x.transpose(0, 2, 1, 3).reshape(b * n, t, f)
        out = _mamba(seq, W_in, conv_w, conv_b, W_x, W_dt, b_dt, A_log, Dp, W_out)
        return out.reshape(b, n, t, f).transpose(0, 2, 1, 3)

    def _L2_conv_ref(x, conv_w, W1, b1, W2, b2, out_w, tau):
        import jax, jax.numpy as jnp
        import numpy as np
        N = 64
        CH = 128
        RES = 64
        LRF = 4
        LH = RES // LRF
        LW = RES // LRF
        L = LH * LW
        K = max(1, int(L * 0.1))
        NB = LRF * LRF
        OC = CH // 10 + 1
        INDIM = K * CH + L
        HID = INDIM
        OUTDIM = L * OC
        n, c, H, W = x.shape
        xb = x.reshape(n, c, LRF, LH, LRF, LW).transpose(2, 4, 0, 1, 3, 5)
        xb = xb.reshape(NB, n, c, L)
        scores = jnp.einsum('gbcl,gc->gbl', xb, conv_w)
        e = jnp.exp(scores)
        p = e / jnp.sum(e, axis=-1, keepdims=True)
        _, idx = jax.lax.top_k(p, K)
        mask = jnp.sum(jax.nn.one_hot(idx, L, dtype=p.dtype), axis=2)
        st = jax.lax.stop_gradient(mask - p) + p
        out = st[:, :, None, :] * xb
        idx_s = jnp.sort(idx, axis=-1)
        gath = jnp.take_along_axis(out, idx_s[:, :, None, :], axis=-1)
        feat = jnp.concatenate([gath.transpose(0, 1, 3, 2).reshape(NB, n, K * c), st], axis=-1)
        h = jax.nn.relu(feat @ W1 + b1)
        rec = (h @ W2 + b2).reshape(NB, n, OC, LH, LW)
        grid = rec.reshape(LRF, LRF, n, OC, LH, LW).transpose(2, 3, 0, 4, 1, 5)
        grid = grid.reshape(n, OC, H, W)
        return jnp.einsum('bohw,co->bchw', grid, out_w)

    def _L3_conv_ref(x):
        import jax, jax.numpy as jnp
        import numpy as np

        def _avg_pool(x, s):
            if s == 1:
                return x
            B, C, H, W = x.shape
            return x.reshape(B, C, H // s, s, W // s, s).mean(axis=(3, 5))

        def _attention(x):
            B, C, H, W = x.shape
            xf = x.reshape(B, C, H * W)
            scores = jnp.einsum('bcn,bcm->bnm', xf, xf)
            attn = jax.nn.softmax(scores, axis=-1)
            out = jnp.einsum('bnm,bcm->bcn', attn, xf)
            return out.reshape(B, C, H, W)
        B, C, H, W = x.shape
        out = jnp.zeros_like(x)
        for scale in (4, 2, 1):
            block = _avg_pool(x, scale)
            block = _attention(block)
            block = jax.image.resize(block, (B, C, H, W), method='bilinear')
            out = out + block
        return out

    def _gn(v, G=32, eps=1e-5):
        B_, H_, W_, C_ = v.shape
        g = v.reshape(B_, H_, W_, G, C_ // G)
        m = jnp.mean(g, axis=(1, 2, 4), keepdims=True)
        s = jnp.var(g, axis=(1, 2, 4), keepdims=True)
        return ((g - m) / jnp.sqrt(s + eps)).reshape(v.shape)

    def _ln_c(v, eps=1e-6):
        m = jnp.mean(v, axis=-1, keepdims=True)
        s = jnp.var(v, axis=-1, keepdims=True)
        return (v - m) / jnp.sqrt(s + eps)

    def _ln_t(v, eps=1e-5):
        m = jnp.mean(v, axis=-1, keepdims=True)
        s = jnp.var(v, axis=-1, keepdims=True)
        return (v - m) / jnp.sqrt(s + eps)

    def _to_tokens(v):
        B_, H_, W_, C_ = v.shape
        return v.reshape(B_, H_ * W_, C_)
    def _from_tokens(t, like):
        return t.reshape(like.shape)

    x = x + _L0_conv_ref(_gn(x), L0_conv_W_in, L0_conv_conv_w, L0_conv_conv_b, L0_conv_W_x, L0_conv_W_dt, L0_conv_b_dt, L0_conv_A_log, L0_conv_Dp, L0_conv_W_out)
    x = x + _L1_conv_ref(_gn(x), L1_conv_W_in, L1_conv_conv_w, L1_conv_conv_b, L1_conv_W_x, L1_conv_W_dt, L1_conv_b_dt, L1_conv_A_log, L1_conv_Dp, L1_conv_W_out)
    x = x + _L2_conv_ref(_gn(x), L2_conv_conv_w, L2_conv_W1, L2_conv_b1, L2_conv_W2, L2_conv_b2, L2_conv_out_w, 1)
    x = x + _L3_conv_ref(_gn(x))
    return x


_drawn_inputs = setup_inputs


def setup_inputs(seed=0):
    import zlib

    import numpy as np

    out = dict(_drawn_inputs(seed))
    spreads = {'L0_conv_conv_b': (0.0, 0.1),
     'L0_conv_Dp': (1.0, 0.6),
     'L1_conv_conv_b': (0.0, 0.1),
     'L1_conv_Dp': (1.0, 0.6),
     'L2_conv_b1': (0.0, 0.556),
     'L2_conv_b2': (0.0, 0.469)}
    factors = {'L0_conv_conv_w': 8.0,
     'L0_conv_W_x': 8.0,
     'L0_conv_W_dt': 8.0,
     'L0_conv_b_dt': 8.0,
     'L0_conv_A_log': 8.0,
     'L0_conv_W_out': 2.71,
     'L1_conv_W_in': 3.485,
     'L1_conv_conv_w': 8.0,
     'L1_conv_W_x': 8.0,
     'L1_conv_W_dt': 8.0,
     'L1_conv_b_dt': 8.0,
     'L1_conv_A_log': 8.0,
     'L1_conv_W_out': 3.933}
    for name, (base, spread) in spreads.items():
        noise = np.random.default_rng([zlib.crc32(name.encode()), seed]).standard_normal(out[name].shape)
        drawn = base * np.exp(spread * noise) if base else spread * noise
        out[name] = jnp.asarray(drawn.astype(out[name].dtype))
    for name, factor in factors.items():
        out[name] = (out[name] * factor).astype(out[name].dtype)
    return out
```

```python
import concourse.bass as bass
from concourse import mybir
from contextlib import ExitStack

fp32 = mybir.dt.float32
fp16 = mybir.dt.float16
bf16 = mybir.dt.bfloat16
ALU = mybir.AluOpType
ACT = mybir.ActivationFunctionType
AX = mybir.AxisListType
EXP_LN_TABLES = "natural_log_exp_and_others"

P = 128
B, T, N, F = 4, 128, 64, 64
PIX = N * F
G = F // 2
D = 128
S = 16
R = 4
TAPS = 4
BANK = 512


def wait(eng, sem, value):
    if isinstance(value, int) and value <= 0:
        return
    eng.wait_ge(sem, value)


class Memory:

    def __init__(self, nc, tag):
        self.nc, self.tag, self.stack = nc, tag, ExitStack()

    def __enter__(self):
        self.stack.__enter__()
        return self

    def __exit__(self, *e):
        return self.stack.__exit__(*e)

    def sb(self, name, shape, dt=fp32):
        return self.stack.enter_context(self.nc.sbuf_tensor(f"{self.tag}_{name}", shape, dt))

    def ps(self, name, shape, dt=fp32):
        return self.stack.enter_context(self.nc.psum_tensor(f"{self.tag}_{name}", shape, dt))


class Semaphores:

    def __init__(self, nc):
        self.nc, self.stack, self.taken = nc, ExitStack(), []

    def __call__(self, name):
        self.taken.append(self.stack.enter_context(self.nc.semaphore(name)))
        return self.taken[-1]

    def __enter__(self):
        self.stack.__enter__()
        return self

    def __exit__(self, *e):
        with self.nc.Block() as block:
            @block.sync
            def _(sp):
                for s in self.taken:
                    sp.sem_clear(s)
        return self.stack.__exit__(*e)


def group_norm_stats(nc, sem, tag, X, C, scale_g, bias_g):
    with Memory(nc, tag) as m:
        stats = m.sb("stats", [P, B * G * 6])
        pair_sum = m.sb("pair_sum", [P, B * G])
        diff = m.sb("diff", [P, B * G])
        square = m.sb("square", [P, B * G])
        spread = m.sb("spread", [P, B * G])
        dev = m.sb("dev", [P, B * G])
        var = m.sb("var", [P, B * G])
        root = m.sb("root", [P, B * G])
        mean_ps = m.ps("mean_ps", [P, BANK])
        var_ps = m.ps("var_ps", [P, BANK])
        s_stats = sem(f"{tag}_bn_stats_done")
        s_chain = sem(f"{tag}_vector_step")
        s_mean = sem(f"{tag}_mean_ready")
        s_var = sem(f"{tag}_var_ready")
        s_root = sem(f"{tag}_root_ready")
        Xv = X[:, :].rearrange("p (b n f) -> p b n f", b=B, n=N)
        count_half = N
        with nc.Block() as block:
            @block.vector
            def _(dve):
                with dve.Fori(0, G) as g:
                    for b in range(B):
                        nc.vector.bn_stats(out=stats[:, bass.ds(g * 6 + b * G * 6, 6)],
                                           in_=Xv[:, b, :, bass.ds(g * 2, 2)]).then_inc(s_stats, 1)
                dve.wait_ge(s_stats, B * G)
                steps = [0]

                def step(ins):
                    steps[0] += 1
                    ins.then_inc(s_chain, 1)
                    dve.wait_ge(s_chain, steps[0])

                st = stats[:, :].rearrange("p (g k) -> p g k", k=6)
                nc.vector.tensor_tensor(diff[:, :], st[:, :, 1], st[:, :, 4], ALU.subtract)
                nc.vector.tensor_tensor(spread[:, :], st[:, :, 2], st[:, :, 5], ALU.add)
                step(nc.vector.tensor_tensor(pair_sum[:, :], st[:, :, 1], st[:, :, 4], ALU.add))
                step(nc.vector.tensor_tensor(square[:, :], diff[:, :], diff[:, :], ALU.mult))
                step(nc.vector.scalar_tensor_tensor(spread[:, :], square[:, :], count_half / 2.0,
                                                    spread[:, :], ALU.mult, ALU.add))
                dve.wait_ge(s_mean, 1)
                step(nc.vector.scalar_tensor_tensor(dev[:, :], pair_sum[:, :], 0.5, mean_ps[:, 0:B * G],
                                                    ALU.mult, ALU.subtract))
                step(nc.vector.tensor_tensor(square[:, :], dev[:, :], dev[:, :], ALU.mult))
                step(nc.vector.scalar_tensor_tensor(spread[:, :], square[:, :], 2.0 * count_half,
                                                    spread[:, :], ALU.mult, ALU.add))
                dve.wait_ge(s_var, 1)
                step(nc.vector.tensor_scalar(var[:, :], var_ps[:, 0:B * G], 1e-5, None, ALU.add))
                dve.wait_ge(s_root, 1)
                step(nc.vector.reciprocal(root[:, :], root[:, :]))
                step(nc.vector.tensor_tensor(square[:, :], root[:, :], root[:, :], ALU.mult))
                step(nc.vector.tensor_tensor(square[:, :], square[:, :], var[:, :], ALU.mult))
                step(nc.vector.tensor_scalar(square[:, :], square[:, :], -0.5, 1.5, ALU.mult, ALU.add))
                step(nc.vector.tensor_tensor(scale_g[:, :], root[:, :], square[:, :], ALU.mult))
                step(nc.vector.scalar_tensor_tensor(bias_g[:, :], mean_ps[:, 0:B * G], -1.0, scale_g[:, :],
                                                    ALU.mult, ALU.mult))

            @block.tensor
            def _(pe):
                pe.wait_ge(s_chain, 1)
                nc.tensor.matmul(mean_ps[:, 0:B * G], C["mean_of_pairs"][:, :], pair_sum[:, :],
                                 start=True, stop=True).then_inc(s_mean, 1)
                pe.wait_ge(s_chain, 6)
                nc.tensor.matmul(var_ps[:, 0:B * G], C["mean_of_sums"][:, :], spread[:, :],
                                 start=True, stop=True).then_inc(s_var, 1)

            @block.scalar
            def _(act):
                act.wait_ge(s_chain, 7)
                nc.scalar.activation(root[:, :], var[:, :], ACT.Sqrt).then_inc(s_root, 1)


def mamba_weights(nc, sem, tag, W, C, M):
    with Memory(nc, tag + "w") as m:
        w_in = m.sb("w_in", [P, 2, F])
        cw = m.sb("cw", [P, TAPS])
        wx = m.sb("wx", [R + 2 * S, D])
        wdt = m.sb("wdt", [P, R])
        wout = m.sb("wout", [F, D])
        dp = m.sb("dp", [P, 1])
        cb = m.sb("cb", [P, 1])
        taps = m.sb("taps", [P, TAPS + 1, 2, F])
        wdt_t = m.sb("wdt_t", [R, D])
        tap_ps = m.ps("tap_ps", [P, TAPS * D])
        z_ps = m.ps("z_ps", [P, BANK])
        x_ps = m.ps("x_ps", [P, BANK])
        dt_ps = m.ps("dt_ps", [P, BANK])
        out_ps = m.ps("out_ps", [P, BANK])
        f_ps = m.ps("f_ps", [P, BANK])
        s_load = sem(f"{tag}_weights_loaded")
        s_taps = sem(f"{tag}_taps_scaled")
        s_turn = sem(f"{tag}_weights_transposed")
        s_wdt = sem(f"{tag}_wdt_copied")
        s_fused = sem(f"{tag}_dt_product")
        s_exp = sem(f"{tag}_a_exp")
        with nc.Block() as block:
            @block.sync
            def _(sp):
                col = lambda a: a.rearrange("(p o) -> p o", o=1)
                sp.dma_start(w_in[:, :, :], W["W_in"].rearrange("(h p) f -> p h f", p=P)).then_inc(s_load, 16)
                sp.dma_start(cw[:, :], W["conv_w"]).then_inc(s_load, 16)
                sp.dma_start(wx[:, :], W["W_x"]).then_inc(s_load, 16)
                sp.dma_start(wdt[:, :], W["W_dt"]).then_inc(s_load, 16)
                sp.dma_start(wout[:, :], W["W_out"]).then_inc(s_load, 16)
                sp.dma_start(dp[:, :], col(W["Dp"])).then_inc(s_load, 16)
                sp.dma_start(M["conv_b"][:, :], col(W["conv_b"])).then_inc(s_load, 16)
                sp.dma_start(M["b_dt"][:, :], col(W["b_dt"])).then_inc(s_load, 16)
                sp.dma_start(M["A"][:, :], W["A_log"]).then_inc(s_load, 16)

            @block.scalar
            def _(act):
                act.wait_ge(s_load, 9 * 16)
                nc.scalar.activation(M["A"][:, :], M["A"][:, :], ACT.Exp).then_inc(s_exp, 1)

            @block.vector
            def _(dve):
                dve.wait_ge(s_load, 9 * 16)
                for copy in range(2):
                    for k in range(TAPS):
                        nc.vector.tensor_scalar(taps[:, k, copy, :], w_in[:, 0, :], cw[:, k:k + 1], None,
                                                ALU.mult).then_inc(s_taps, 1)
                    nc.vector.tensor_copy(taps[:, TAPS, copy, :], w_in[:, 1, :]).then_inc(s_taps, 1)
                nc.vector.tensor_scalar(M["neg_conv_b"][:, :], M["conv_b"][:, :], -1.0, None, ALU.mult)
                nc.vector.tensor_scalar(M["diag_Dp"][:, :], C["ident"][:, :], dp[:, 0:1], None, ALU.mult)
                dve.wait_ge(s_exp, 1)
                nc.vector.tensor_scalar(M["A"][:, :], M["A"][:, :], -1.0, None, ALU.mult)
                dve.wait_ge(s_turn, 5)
                nc.vector.tensor_copy(wdt_t[:, :], dt_ps[0:R, 0:D]).then_inc(s_wdt, 1)
                nc.vector.tensor_copy(M["taps"][:, 0:TAPS * D], tap_ps[:, :])
                nc.vector.tensor_copy(M["taps"][:, TAPS * D:(TAPS + 1) * D], z_ps[:, 0:D])
                for part in range(3):
                    nc.vector.tensor_copy(M["w_bc"][:, part * 2 * S:(part + 1) * 2 * S], x_ps[:, R:R + 2 * S])
                nc.vector.tensor_copy(M["w_out"][:, :], out_ps[:, 0:F])
                dve.wait_ge(s_fused, 1)
                nc.vector.tensor_copy(M["w_dt"][:, :], f_ps[:, 0:D])

            @block.tensor
            def _(pe):
                pe.wait_ge(s_load, 9 * 16)
                pe.wait_ge(s_taps, 2 * (TAPS + 1))
                ident = C["ident"]
                for k in range(TAPS):
                    last = nc.tensor.transpose(tap_ps[:, k * D:(k + 1) * D],
                                               taps[:, k, :, :].rearrange("p c f -> p (c f)"), ident[:, :])
                last.then_inc(s_turn, 1)
                nc.tensor.transpose(z_ps[:, 0:D], taps[:, TAPS, :, :].rearrange("p c f -> p (c f)"),
                                    ident[:, :]).then_inc(s_turn, 1)
                nc.tensor.transpose(x_ps[:, 0:R + 2 * S], wx[:, :],
                                    ident[0:R + 2 * S, 0:R + 2 * S]).then_inc(s_turn, 1)
                nc.tensor.transpose(dt_ps[0:R, 0:D], wdt[:, :], ident[:, :]).then_inc(s_turn, 1)
                nc.tensor.transpose(out_ps[:, 0:F], wout[:, :], ident[0:F, 0:F]).then_inc(s_turn, 1)
                pe.wait_ge(s_wdt, 1)
                nc.tensor.matmul(f_ps[:, 0:D], wx[0:R, :], wdt_t[:, :], start=True, stop=True).then_inc(s_fused, 1)


def mamba_norm(nc, sem, tag, scale_g, bias_g, C, scale_c, bias_c):
    with Memory(nc, tag + "n") as m:
        rows = m.sb("rows", [1, 2, B, 2, F])
        cols = m.ps("cols", [P, BANK])
        s_rows = sem(f"{tag}_norm_rows")
        s_cols = sem(f"{tag}_norm_cols")
        with nc.Block() as block:
            @block.vector
            def _(dve):
                for k, src in enumerate((scale_g, bias_g)):
                    for copy in range(2):
                        for e in range(2):
                            nc.vector.tensor_copy(
                                rows[0:1, k, :, copy, :].rearrange("p b (g e) -> p b g e", e=2)[:, :, :, e],
                                src[0:1, :].rearrange("p (b g) -> p b g", b=B)).then_inc(s_rows, 1)
                dve.wait_ge(s_cols, 2 * B)
                for k, dst in enumerate((scale_c, bias_c)):
                    nc.vector.tensor_copy(dst[:, :].rearrange("p (b c) -> p b c", b=B),
                                          cols[:, k * B:(k + 1) * B].unsqueeze(2).to_broadcast([P, B, CHUNKS // B]))

            @block.tensor
            def _(pe):
                pe.wait_ge(s_rows, 8)
                for k in range(2):
                    for b in range(B):
                        nc.tensor.matmul(cols[:, k * B + b:k * B + b + 1],
                                         rows[0:1, k, b, :, :].rearrange("p c f -> p (c f)"),
                                         C["one"][0:1, 0:1], start=True, stop=True).then_inc(s_cols, 1)


CHUNK_N = 8
CHUNKS = B * N // CHUNK_N
COLS = CHUNK_N * F
HALF = CHUNK_N // 2 * T
TOK = 2 * HALF
PREP_PE = ["turn"] + [f"{k}{h}" for h in range(2) for k in ("u", "z", "dt", "bc")]
LAG = 2


def mamba_layer(nc, sem, tag, X, C, M, scale_c, bias_c):
    with Memory(nc, tag) as m:
        xs = m.sb("xs", [P, COLS])
        xt = m.sb("xt", [P, COLS])
        u = m.sb("u", [P, 2, TOK])
        dt = m.sb("dt", [P, 2, TOK])
        dtu = m.sb("dtu", [P, 2, TOK])
        sz = m.sb("sz", [P, 2, TOK])
        bc = m.sb("bc", [3 * 2 * S, 2, TOK], bf16)
        rest = m.sb("rest", [3 * 2 * S, HALF])
        eu = m.sb("eu", [P, HALF])
        lu = m.sb("lu", [P, HALF])
        gu = m.sb("gu", [P, HALF])
        ez = m.sb("ez", [P, HALF])
        lz = m.sb("lz", [P, HALF])
        gz = m.sb("gz", [P, HALF])
        mag = m.sb("mag", [P, HALF])
        ed = m.sb("ed", [P, HALF])
        pos = m.sb("pos", [P, HALF])
        one_e = m.sb("one_e", [P, HALF])
        ln_e = m.sb("ln_e", [P, HALF])
        lost = m.sb("lost", [P, HALF])
        log1p = m.sb("log1p", [P, HALF])
        decay = m.sb("decay", [P, 4, TOK])
        drive = m.sb("drive", [P, 2, TOK])
        state = m.sb("state", [P, 2, TOK])
        c_row = m.sb("c_row", [P, 2, TOK])
        hc = m.sb("hc", [P, 2, TOK])
        yz = m.sb("yz", [P, TOK])
        b_ps = [m.ps(f"b_ps{h}", [P, BANK]) for h in range(2)]
        c_ps = [m.ps(f"c_ps{h}", [P, BANK]) for h in range(2)]
        y_ps = [m.ps(f"y_ps{h}", [P, BANK]) for h in range(2)]
        even_ps = m.ps("even_ps", [P, BANK])
        odd_ps = m.ps("odd_ps", [P, BANK])

        s_xs = sem(f"{tag}_xs_loaded")
        s_prep = sem(f"{tag}_prep_product")
        s_xt = sem(f"{tag}_xt_ready")
        s_su = sem(f"{tag}_sigmoid_u")
        s_sz = sem(f"{tag}_sigmoid_z")
        s_u = sem(f"{tag}_u_ready")
        s_szr = sem(f"{tag}_silu_z_ready")
        s_abs = sem(f"{tag}_dt_abs_relu_exp")
        s_one = sem(f"{tag}_one_plus_e")
        s_ln = sem(f"{tag}_ln_ready")
        s_lost = sem(f"{tag}_lost_ready")
        s_log1p = sem(f"{tag}_log1p_ready")
        s_dt = sem(f"{tag}_dt_ready")
        s_dtu = sem(f"{tag}_dtu_ready")
        s_hi = sem(f"{tag}_bc_high")
        s_rest = sem(f"{tag}_bc_rest")
        s_mid = sem(f"{tag}_bc_middle")
        s_lo = sem(f"{tag}_bc_low")
        s_zero = sem(f"{tag}_starts_cleared")
        s_b = sem(f"{tag}_b_row")
        s_c = sem(f"{tag}_c_row")
        s_decay = sem(f"{tag}_decay_ready")
        s_drive = sem(f"{tag}_drive_ready")
        s_scan = sem(f"{tag}_state_ready")
        s_crow = sem(f"{tag}_c_copied")
        s_hc = sem(f"{tag}_hc_ready")
        s_y = sem(f"{tag}_y_summed")
        s_yz = sem(f"{tag}_yz_ready")
        s_out = sem(f"{tag}_out_product")
        s_x = sem(f"{tag}_x_updated")

        NPREP = len(PREP_PE)

        def half(h):
            return slice(h * HALF, (h + 1) * HALF)

        def prep_at(c, name):
            return c * NPREP + PREP_PE.index(name) + 1

        def load_xs(sp, c):
            wait(sp, s_prep, prep_at(c - 1, "turn"))
            sp.dma_start(xs[:, :], X[:, bass.ds(c * COLS, COLS)]).then_inc(s_xs, 16)

        def pe_prep(pe, c, par, k):
            ident = C["ident"]
            if k == 0:
                wait(pe, s_xs, 16 * (c + 1))
                wait(pe, s_rest, 2 * c)
                for j in range(CHUNK_N // 2):
                    last = nc.tensor.transpose(even_ps[:, j * T:(j + 1) * T], xs[:, j * P:(j + 1) * P], ident[:, :])
                last.then_inc(s_prep, 1)
            for h in range(2):
                rows = slice(h * F, (h + 1) * F)
                if k == 2 + 6 * h:
                    if h == 0:
                        wait(pe, s_xt, c + 1)
                        wait(pe, s_x, c - 1)
                    else:
                        wait(pe, s_abs, 3 * (2 * c + h))
                    src = xt[rows, :].rearrange("p (j t) -> p j t", t=T)
                    dst = odd_ps[:, :].rearrange("p (j t) -> p j t", t=T)
                    for tap in reversed(range(TAPS)):
                        back = TAPS - 1 - tap
                        last = nc.tensor.matmul(dst[:, :, back:T], M["taps"][rows, tap * D:(tap + 1) * D],
                                                src[:, :, 0:T - back], start=(back == 0), stop=(tap == 0))
                    last.then_inc(s_prep, 1)
                    if h == 1:
                        wait(pe, s_rest, 2 * c + 1)
                    nc.tensor.matmul(even_ps[:, :], M["taps"][rows, TAPS * D:(TAPS + 1) * D], xt[rows, :],
                                     start=True, stop=True).then_inc(s_prep, 1)
                if k == 5 + 6 * h:
                    wait(pe, s_u, 2 * c + h + 1)
                    nc.tensor.matmul(odd_ps[:, :], M["w_dt"][:, :], u[:, par, half(h)],
                                     start=True, stop=True).then_inc(s_prep, 1)
                    wait(pe, s_szr, 2 * c + h + 1)
                    nc.tensor.matmul(even_ps[0:3 * 2 * S, :], M["w_bc"][:, :], u[:, par, half(h)],
                                     start=True, stop=True).then_inc(s_prep, 1)

        def pe_rows(pe, c, par, s):
            unit = c * S + s
            if s == 0:
                wait(pe, s_lo, 2 * (c + 1))
            for h in range(2):
                wait(pe, s_drive, 2 * unit + h - 1)
                nc.tensor.matmul(b_ps[h][:, :], C["pick"][:, s * P:(s + 1) * P], bc[:, par, half(h)],
                                 start=True, stop=True).then_inc(s_b, 1)
            for h in range(2):
                wait(pe, s_crow, 2 * unit + h - 1)
                nc.tensor.matmul(c_ps[h][:, :], C["pick"][:, (S + s) * P:(S + s + 1) * P], bc[:, par, half(h)],
                                 start=True, stop=True).then_inc(s_c, 1)

        def pe_sum(pe, c, par, s):
            unit = c * S + s
            if s == 0:
                wait(pe, s_yz, 2 * c)
                for h in range(2):
                    nc.tensor.matmul(y_ps[h][:, :], M["diag_Dp"][:, :], u[:, par, half(h)], start=True, stop=False)
            wait(pe, s_hc, unit + 1)
            for h in range(2):
                nc.tensor.matmul(y_ps[h][:, :], C["ident"][:, :], hc[:, s % 2, half(h)],
                                 start=False, stop=(s == S - 1)).then_inc(s_y, 1)

        def pe_out(pe, c, prep):
            wait(pe, s_yz, 2 * (c + 1))
            if prep:
                wait(pe, s_abs, 3 * 2 * (c + 2))
            for h in range(2):
                for j in range(CHUNK_N // 2):
                    n = 2 * j + h
                    last = nc.tensor.matmul(odd_ps[:, n * F:(n + 1) * F], yz[:, h * HALF + j * T:h * HALF + (j + 1) * T],
                                            M["w_out"][:, :], start=True, stop=True)
            last.then_inc(s_out, 1)

        def act_prep(act, c, par, k):
            if k == 1:
                wait(act, s_prep, prep_at(c, "turn"))
                wait(act, s_prep, prep_at(c - 1, "z1"))
                nc.scalar.activation(xt[:, :], even_ps[:, :], ACT.Identity, scale=scale_c[:, bass.ds(c, 1)],
                                     bias=bias_c[:, bass.ds(c, 1)]).then_inc(s_xt, 1)
            for h in range(2):
                n = 2 * c + h
                at = k - 6 * h
                if at == 3:
                    wait(act, s_prep, prep_at(c, f"u{h}"))
                    wait(act, s_su, 3 * n)
                    nc.scalar.activation(eu[:, :], odd_ps[:, :], ACT.Exp, scale=-1.0,
                                         bias=M["neg_conv_b"][:, 0:1]).then_inc(s_su, 1)
                    wait(act, s_prep, prep_at(c, f"z{h}"))
                    wait(act, s_sz, 3 * n)
                    nc.scalar.activation(ez[:, :], even_ps[:, :], ACT.Exp, scale=-1.0).then_inc(s_sz, 1)
                    wait(act, s_su, 3 * n + 1)
                    nc.scalar.activation(lu[:, :], eu[:, :], ACT.Ln, bias=1.0).then_inc(s_su, 1)
                    wait(act, s_su, 3 * n + 2)
                    wait(act, s_u, n)
                    nc.scalar.activation(gu[:, :], lu[:, :], ACT.Exp, scale=-1.0).then_inc(s_su, 1)
                if at == 4:
                    wait(act, s_sz, 3 * n + 1)
                    nc.scalar.activation(lz[:, :], ez[:, :], ACT.Ln, bias=1.0).then_inc(s_sz, 1)
                    wait(act, s_sz, 3 * n + 2)
                    wait(act, s_szr, n)
                    nc.scalar.activation(gz[:, :], lz[:, :], ACT.Exp, scale=-1.0).then_inc(s_sz, 1)
                if at == 6:
                    wait(act, s_prep, prep_at(c, f"dt{h}"))
                    wait(act, s_abs, 3 * n)
                    nc.scalar.activation(mag[:, :], odd_ps[:, :], ACT.Abs, bias=M["b_dt"][:, 0:1]).then_inc(s_abs, 1)
                    wait(act, s_dt, n)
                    nc.scalar.activation(pos[:, :], odd_ps[:, :], ACT.Relu, bias=M["b_dt"][:, 0:1]).then_inc(s_abs, 1)
                    wait(act, s_abs, 3 * n + 1)
                    wait(act, s_lost, n)
                    nc.scalar.activation(ed[:, :], mag[:, :], ACT.Exp, scale=-1.0).then_inc(s_abs, 1)
                    wait(act, s_prep, prep_at(c, f"bc{h}"))
                    if h == 0:
                        wait(act, s_c, 2 * S * (c - 1))
                    nc.scalar.activation(bc[:, par, half(h)], even_ps[0:3 * 2 * S, :], ACT.Copy).then_inc(s_hi, 1)
                if at == 8:
                    wait(act, s_one, n + 1)
                    wait(act, s_log1p, n)
                    nc.scalar.activation(ln_e[:, :], one_e[:, :], ACT.Ln).then_inc(s_ln, 1)
                    wait(act, s_rest, n + 1)
                    wait(act, s_hi, n + 1)
                    nc.scalar.activation(bc[2 * S:4 * S, par, half(h)], rest[2 * S:4 * S, :], ACT.Copy)
                    nc.scalar.activation(bc[4 * S:6 * S, par, half(h)], rest[4 * S:6 * S, :], ACT.Copy).then_inc(s_mid, 1)

        def act_unit(act, c, par, s):
            unit = c * S + s
            if s == 0:
                wait(act, s_dt, 2 * (c + 1))
                wait(act, s_zero, 4)
            wait(act, s_scan, unit - 3)
            seq = lambda a: a.rearrange("p (q t) -> p q t", t=T)[:, :, 1:T]
            nc.scalar.activation(seq(decay[:, s % 4, :]), seq(dt[:, par, :]), ACT.Exp,
                                 scale=M["A"][:, s:s + 1]).then_inc(s_decay, 1)
            for h in range(2):
                wait(act, s_c, 2 * unit + h + 1)
                if h == 0:
                    wait(act, s_hc, unit - 1)
                nc.scalar.activation(c_row[:, s % 2, half(h)], c_ps[h][:, :], ACT.Copy).then_inc(s_crow, 1)

        def dve_prep(dve, c, par, k):
            for h in range(2):
                n = 2 * c + h
                at = k - 6 * h
                if at == 4:
                    wait(dve, s_su, 3 * n + 3)
                    if h == 0:
                        wait(dve, s_y, 2 * (S * (c - 2) + 1))
                        wait(dve, s_dtu, 2 * (c - 1))
                    nc.vector.scalar_tensor_tensor(u[:, par, half(h)], odd_ps[:, :], M["conv_b"][:, 0:1],
                                                   gu[:, :], ALU.add, ALU.mult).then_inc(s_u, 1)
                if at == 5:
                    wait(dve, s_sz, 3 * n + 3)
                    if h == 0:
                        wait(dve, s_yz, 2 * (c - 1))
                    nc.vector.tensor_tensor(sz[:, par, half(h)], even_ps[:, :], gz[:, :], ALU.mult).then_inc(s_szr, 1)
                if at == 7:
                    wait(dve, s_abs, 3 * n + 3)
                    wait(dve, s_ln, n)
                    wait(dve, s_lost, n)
                    nc.vector.tensor_scalar(one_e[:, :], ed[:, :], 1.0, None, ALU.add).then_inc(s_one, 1)
                    wait(dve, s_hi, n + 1)
                    wait(dve, s_lo, n)
                    nc.vector.tensor_tensor(rest[2 * S:4 * S, :], even_ps[2 * S:4 * S, :],
                                            bc[2 * S:4 * S, par, half(h)], ALU.subtract)
                    nc.vector.tensor_tensor(rest[4 * S:6 * S, :], even_ps[4 * S:6 * S, :],
                                            bc[4 * S:6 * S, par, half(h)], ALU.subtract).then_inc(s_rest, 1)
                    wait(dve, s_one, n + 1)
                    wait(dve, s_log1p, n)
                    nc.vector.scalar_tensor_tensor(lost[:, :], one_e[:, :], -1.0, ed[:, :],
                                                   ALU.add, ALU.subtract).then_inc(s_lost, 1)
                if at == 8:
                    wait(dve, s_ln, n + 1)
                    wait(dve, s_lost, n + 1)
                    wait(dve, s_dt, n)
                    nc.vector.tensor_tensor(log1p[:, :], ln_e[:, :], lost[:, :], ALU.subtract).then_inc(s_log1p, 1)
                    wait(dve, s_mid, n + 1)
                    nc.vector.tensor_tensor(bc[4 * S:6 * S, par, half(h)], rest[4 * S:6 * S, :],
                                            bc[4 * S:6 * S, par, half(h)], ALU.subtract).then_inc(s_lo, 1)

        def dve_drive(dve, c, par, s):
            unit = c * S + s
            if s == 0:
                wait(dve, s_dtu, 2 * (c + 1))
            wait(dve, s_scan, unit - 1)
            for h in range(2):
                wait(dve, s_b, 2 * unit + h + 1)
                nc.vector.tensor_tensor(drive[:, s % 2, half(h)], dtu[:, par, half(h)], b_ps[h][:, :],
                                        ALU.mult).then_inc(s_drive, 1)

        def dve_scan(dve, c, par, s):
            unit = c * S + s
            wait(dve, s_decay, unit + 1)
            wait(dve, s_drive, 2 * unit + 2)
            wait(dve, s_hc, unit - 1)
            nc.vector.tensor_tensor_scan(state[:, s % 2, :], decay[:, s % 4, :], drive[:, s % 2, :], 0.0,
                                         ALU.mult, ALU.add).then_inc(s_scan, 1)

        def dve_gate(dve, c, par):
            for h in range(2):
                wait(dve, s_y, 2 * S * c + 2 * (S - 1) + h + 1)
                wait(dve, s_out, c)
                nc.vector.tensor_tensor(yz[:, half(h)], sz[:, par, half(h)], y_ps[h][:, :],
                                        ALU.mult).then_inc(s_yz, 1)

        def dve_add(dve, c):
            wait(dve, s_out, c + 1)
            nc.vector.tensor_tensor(X[:, bass.ds(c * COLS, COLS)], X[:, bass.ds(c * COLS, COLS)], odd_ps[:, :],
                                    ALU.add).then_inc(s_x, 1)

        def pool_prep(pool, c, par, k):
            for h in range(2):
                n = 2 * c + h
                if k - 6 * h == 9:
                    wait(pool, s_log1p, n + 1)
                    if h == 0:
                        wait(pool, s_decay, S * (c - 1))
                        wait(pool, s_drive, 2 * S * (c - 1))
                    nc.gpsimd.tensor_tensor(dt[:, par, half(h)], log1p[:, :], pos[:, :], ALU.add).then_inc(s_dt, 1)
                    wait(pool, s_dt, n + 1)
                    wait(pool, s_u, n + 1)
                    nc.gpsimd.tensor_tensor(dtu[:, par, half(h)], dt[:, par, half(h)], u[:, par, half(h)],
                                            ALU.mult).then_inc(s_dtu, 1)

        def pool_unit(pool, c, par, s):
            unit = c * S + s
            wait(pool, s_scan, unit + 1)
            wait(pool, s_crow, 2 * unit + 2)
            wait(pool, s_y, 2 * (unit - 1))
            nc.gpsimd.tensor_tensor(hc[:, s % 2, :], state[:, s % 2, :], c_row[:, s % 2, :],
                                    ALU.mult).then_inc(s_hc, 1)

        def chunk_units(eng, unit_step, prep_step, c, par, prep):
            for s in range(S):
                unit_step(eng, c, par, s)
                if prep:
                    prep_step(eng, c + 1, 1 - par, s)

        def pe_unit(pe, c, par, s):
            pe_rows(pe, c, par, s)
            first = isinstance(c, int) and c == 0
            if s >= LAG:
                pe_sum(pe, c, par, s - LAG)
            elif not first:
                pe_sum(pe, c - 1, 1 - par, S - LAG + s)
                if s == LAG - 1:
                    pe_out(pe, c - 1, True)

        def dve_unit(dve, c, par, s):
            dve_drive(dve, c, par, s)
            dve_scan(dve, c, par, s)
            first = isinstance(c, int) and c == 0
            if not first:
                if s == LAG - 1:
                    dve_gate(dve, c - 1, 1 - par)
                if s == LAG:
                    dve_add(dve, c - 1)

        def run(eng, unit_step, prep_step):
            chunk_units(eng, unit_step, prep_step, 0, 0, True)
            with eng.Fori(0, (CHUNKS - 2) // 2) as i:
                chunk_units(eng, unit_step, prep_step, 2 * i + 1, 1, True)
                chunk_units(eng, unit_step, prep_step, 2 * i + 2, 0, True)
            chunk_units(eng, unit_step, prep_step, CHUNKS - 1, 1, False)

        last = CHUNKS - 1
        with nc.Block() as block:
            @block.sync
            def _(sp):
                load_xs(sp, 0)
                with sp.Fori(0, CHUNKS - 1) as i:
                    load_xs(sp, i + 1)
                sp.wait_ge(s_xs, 16 * CHUNKS)

            @block.tensor
            def _(pe):
                for k in range(S):
                    pe_prep(pe, 0, 0, k)
                run(pe, pe_unit, pe_prep)
                for s in range(S - LAG, S):
                    pe_sum(pe, last, 1, s)
                pe_out(pe, last, False)

            @block.scalar
            def _(act):
                act.preload_act_table_set(EXP_LN_TABLES)
                for k in range(S):
                    act_prep(act, 0, 0, k)
                run(act, act_unit, act_prep)

            @block.vector
            def _(dve):
                for k in range(S):
                    dve_prep(dve, 0, 0, k)
                run(dve, dve_unit, dve_prep)
                dve_gate(dve, last, 1)
                dve_add(dve, last)

            @block.gpsimd
            def _(pool):
                for slot in range(4):
                    nc.gpsimd.memset(decay[:, slot, :].rearrange("p (q t) -> p q t", t=T)[:, :, 0:1],
                                     0.0).then_inc(s_zero, 1)
                for k in range(S):
                    pool_prep(pool, 0, 0, k)
                run(pool, pool_unit, pool_prep)


GRID = 4
SIDE = N // GRID
L = SIDE * SIDE
ROWS = GRID * GRID * B
TOP = L // 10
OC = P // 10 + 1
HID = TOP * P + L
KT = HID // P
OUT = L * OC
WCOLS = 4 * BANK
WSLOTS = 4
ROWS_PER_BANK = 16


def top_blocks(nc, sem, tag, X, C, W, scale_g, bias_g):
    with Memory(nc, tag) as m:
        xn = m.sb("xn", [P, B * PIX])
        shared = m.sb("shared", [P, HID])
        ring = m.sb("ring", [P, WSLOTS, WCOLS])
        feat = m.sb("feat", [P, KT, ROWS])
        small = m.sb("small", [P, 3 * P])
        ex = m.sb("ex", [ROWS, L])
        prob = m.sb("prob", [ROWS, L])
        left = m.sb("left", [ROWS, 2, L])
        mask = m.sb("mask", [ROWS, L])
        place = m.sb("place", [ROWS, L])
        keep = m.sb("keep", [ROWS, L])
        best = m.sb("best", [ROWS, 4, 8])
        total = m.sb("total", [ROWS, 4])
        place_t = m.sb("place_t", [P, 2, ROWS])
        xt = m.sb("xt", [P, 4, 2, P])
        count = m.sb("count", [P, TOP])
        per_col = m.sb("per_col", [P, 2, B * F])
        shift = shared[:, 0:16 * (2 * ROWS - 1)].rearrange("p (g k) -> p g k", g=16)
        picker = shared[:, 0:2 * ROWS * TOP].rearrange("p (a r k) -> p a r k", a=2, r=ROWS)
        rec = shared[0:ROWS, 0:OUT]
        hidden = xn[0:ROWS, 0:HID]
        hidden_t = xn[:, HID:HID + KT * ROWS].rearrange("p (k r) -> p k r", k=KT)
        b1 = xn[0:1, 6144:6144 + HID]
        b2 = xn[0:1, 10240:10240 + OUT]
        conv_w = small[0:GRID * GRID, 0:P]
        out_w = small[:, P:P + OC]
        out_wt = small[0:OC, 2 * P:3 * P]

        s_ring = [sem(f"{tag}_weight_tile_loaded_{i}") for i in range(WSLOTS)]
        s_used = sem(f"{tag}_weight_tile_used")
        tiles = [(w, k, c) for w in ("W1", "W2") for k in range(KT) for c in range(2)]

        def load_tile(sp, i):
            w, k, c = tiles[i]
            wait(sp, s_used, i - WSLOTS + 1)
            width = (HID, OUT)[w == "W2"]
            lo, hi = c * WCOLS, min((c + 1) * WCOLS, width)
            sp.dma_start(ring[:, i % WSLOTS, 0:hi - lo], W[w][k * P:(k + 1) * P, lo:hi],
                         max_dma_last_dim=8192).then_inc(s_ring[i % WSLOTS], 16)

        with Memory(nc, tag + "a") as a:
            score_ps = a.ps("score_ps", [P, BANK])
            turn_ps = a.ps("turn_ps", [P, BANK])
            xt_ps = [a.ps(f"xt_ps{i}", [P, BANK]) for i in range(2)]
            pick_ps = [a.ps(f"pick_ps{i}", [P, BANK]) for i in range(4)]
            s_load = sem(f"{tag}_small_loaded")
            s_w = sem(f"{tag}_small_turned")
            s_clear = sem(f"{tag}_shift_cleared")
            s_shift = sem(f"{tag}_shift_ready")
            s_mul = sem(f"{tag}_x_scaled")
            s_xn = sem(f"{tag}_x_normed")
            s_score = sem(f"{tag}_scores_ready")
            s_exp = sem(f"{tag}_exp_ready")
            s_step = sem(f"{tag}_choice_step")
            s_turn = sem(f"{tag}_choice_turned")
            s_pick = sem(f"{tag}_picker_ready")
            s_xt = sem(f"{tag}_block_turned")
            s_xtc = [sem(f"{tag}_{k}_pair_copied") for k in ("even", "odd")]
            s_feat = sem(f"{tag}_pixels_picked")
            with nc.Block() as block:
                @block.sync
                def _(sp):
                    sp.dma_start(conv_w, W["conv_w"]).then_inc(s_load, 16)
                    sp.dma_start(out_w, W["out_w"]).then_inc(s_load, 16)
                    for i in range(WSLOTS):
                        load_tile(sp, i)

                @block.gpsimd
                def _(pool):
                    nc.gpsimd.memset(shift, 0.0).then_inc(s_clear, 1)

                @block.scalar
                def _(act):
                    act.preload_act_table_set(EXP_LN_TABLES)
                    act.wait_ge(s_score, 1)
                    nc.scalar.activation(ex[:, :], score_ps[0:ROWS, 0:L], ACT.Exp,
                                         accum_out=total[:, 0:1]).then_inc(s_exp, 1)
                    for i in range(0, ROWS // 2, 2):
                        act.wait_ge(s_xt, i + 1)
                        wait(act, s_feat, i - 1)
                        nc.scalar.activation(xt[:, i % 2 * 2:i % 2 * 2 + 2, :, :].rearrange("p a b c -> p (a b c)"),
                                             xt_ps[i % 2][:, :], ACT.Copy).then_inc(s_xtc[0], 1)

                @block.vector
                def _(dve):
                    n_step = [0]

                    def step(ins):
                        n_step[0] += 1
                        ins.then_inc(s_step, 1)
                        dve.wait_ge(s_step, n_step[0])

                    for e in range(2):
                        for k, src in enumerate((scale_g, bias_g)):
                            nc.vector.tensor_copy(per_col[:, k, :].rearrange("p (g e) -> p g e", e=2)[:, :, e],
                                                  src[:, :]).then_inc(s_mul, 1)
                    xn_v = xn[:, :].rearrange("p (i j n h w) -> p i n h j w", i=GRID, j=GRID, n=B, h=SIDE)
                    x_v = X[:, :].rearrange("p (n i h j w) -> p i n h j w", n=B, i=GRID, h=SIDE, j=GRID)
                    col_v = per_col[:, :, :].rearrange("p k (n j w) -> p k n j w", n=B, j=GRID)
                    col = lambda k, n: col_v[:, k, n, :, :].unsqueeze(1).to_broadcast([P, SIDE, GRID, SIDE])
                    dve.wait_ge(s_w, 2)
                    dve.wait_ge(s_clear, 1)
                    nc.vector.tensor_copy(shift[:, :, ROWS - 1], turn_ps[:, 0:16]).then_inc(s_shift, 1)
                    nc.vector.tensor_copy(out_wt, turn_ps[0:OC, P:2 * P]).then_inc(s_shift, 1)
                    dve.wait_ge(s_mul, 4)
                    for n in range(B):
                        for i in range(GRID):
                            nc.vector.tensor_tensor(xn_v[:, i, n], x_v[:, i, n], col(0, n), ALU.mult).then_inc(s_mul, 1)
                    for n in range(B):
                        for i in range(GRID):
                            dve.wait_ge(s_mul, 4 + n * GRID + i + 1)
                            nc.vector.tensor_tensor(xn_v[:, i, n], xn_v[:, i, n], col(1, n), ALU.add).then_inc(s_xn, 1)
                    dve.wait_ge(s_exp, 1)
                    step(nc.vector.reciprocal(total[:, 1:2], total[:, 0:1]))
                    step(nc.vector.tensor_scalar(prob[:, :], ex[:, :], total[:, 1:2], None, ALU.mult))
                    src = prob[:, :]
                    for k in range(4):
                        step(nc.vector.max(best[:, k, :], src))
                        if k < 3:
                            step(nc.vector.match_replace(out=left[:, k % 2, :], in_to_replace=best[:, k, :],
                                                         in_values=src, imm_value=-1.0))
                            src = left[:, k % 2, :]
                    edge = best[:, (TOP - 1) // 8, (TOP - 1) % 8:(TOP - 1) % 8 + 1]
                    above, equal, ones = mask[:, :], place[:, :], left[:, 0, :]
                    rank = left[:, 1, :]
                    step(nc.vector.tensor_scalar(above, prob[:, :], edge, None, ALU.is_gt))
                    step(nc.vector.tensor_reduce(total[:, 2:3], above, axis=AX.X, op=ALU.add))
                    step(nc.vector.tensor_scalar(total[:, 3:4], total[:, 2:3], -1.0, float(TOP), ALU.mult, ALU.add))
                    step(nc.vector.tensor_scalar(equal, prob[:, :], edge, None, ALU.is_equal))
                    step(nc.vector.memset(ones, 1.0))
                    step(nc.vector.tensor_tensor_scan(rank, ones, equal, 0.0, ALU.mult, ALU.add))
                    step(nc.vector.tensor_scalar(keep[:, :], rank, total[:, 3:4], None, ALU.is_le))
                    step(nc.vector.tensor_tensor(keep[:, :], keep[:, :], equal, ALU.mult))
                    step(nc.vector.tensor_tensor(mask[:, :], above, keep[:, :], ALU.add))
                    step(nc.vector.tensor_tensor_scan(rank, ones, mask[:, :], 0.0, ALU.mult, ALU.add))
                    step(nc.vector.tensor_tensor(place[:, :], rank, mask[:, :], ALU.mult))
                    step(nc.vector.tensor_tensor(keep[:, :], mask[:, :], prob[:, :], ALU.subtract))
                    nc.vector.tensor_tensor(keep[:, :], keep[:, :], prob[:, :], ALU.add).then_inc(s_pick, 1)
                    step(nc.vector.memset(count[:, :], 1.0))
                    ones_l = C["one"][:, 0:TOP]
                    step(nc.vector.tensor_tensor_scan(count[:, :], ones_l, ones_l, 0.0, ALU.mult, ALU.add))
                    dve.wait_ge(s_turn, 1)
                    nc.vector.tensor_copy(feat[:, KT - 2:KT, :],
                                          turn_ps[:, 2 * ROWS:4 * ROWS].rearrange("p (a r) -> p a r", a=2))
                    step(nc.vector.tensor_copy(place_t[:, :, :],
                                               turn_ps[:, 0:2 * ROWS].rearrange("p (a r) -> p a r", a=2)))
                    for h in range(2):
                        step(nc.vector.tensor_tensor(
                            picker[:, h, :, :], count[:, :].unsqueeze(1).to_broadcast([P, ROWS, TOP]),
                            place_t[:, h, :].unsqueeze(2).to_broadcast([P, ROWS, TOP]), ALU.is_equal))
                        nc.vector.tensor_tensor(
                            picker[:, h, :, :], picker[:, h, :, :],
                            feat[:, KT - 2 + h, :].unsqueeze(2).to_broadcast([P, ROWS, TOP]), ALU.mult).then_inc(s_pick, 1)
                    for i in range(1, ROWS // 2, 2):
                        dve.wait_ge(s_xt, i + 1)
                        wait(dve, s_feat, i - 1)
                        nc.vector.tensor_copy(xt[:, 2:4, :, :].rearrange("p a b c -> p (a b c)"),
                                              xt_ps[1][:, :]).then_inc(s_xtc[1], 1)
                    dve.wait_ge(s_feat, ROWS // 2)
                    for q in range(4):
                        rows = slice(q * ROWS_PER_BANK, (q + 1) * ROWS_PER_BANK)
                        nc.vector.tensor_copy(feat[:, 0:TOP, rows].rearrange("p k r -> p r k"),
                                              pick_ps[q][:, 0:ROWS_PER_BANK * TOP].rearrange("p (r k) -> p r k", k=TOP))

                @block.tensor
                def _(pe):
                    ident = C["ident"]
                    pe.wait_ge(s_load, 32)
                    nc.tensor.transpose(turn_ps[:, 0:16], conv_w, ident[0:16, 0:16]).then_inc(s_w, 1)
                    nc.tensor.transpose(turn_ps[0:OC, P:2 * P], out_w, ident[:, :]).then_inc(s_w, 1)
                    pe.wait_ge(s_shift, 2)
                    for n in range(B):
                        pe.wait_ge(s_xn, GRID * (n + 1))
                        for g in range(GRID * GRID):
                            r = g * B + n
                            last = nc.tensor.matmul(score_ps[0:ROWS, 0:L], shift[:, g, ROWS - 1 - r:2 * ROWS - 1 - r],
                                                    xn[:, r * L:(r + 1) * L], start=(n == 0 and g == 0),
                                                    stop=(n == B - 1 and g == 15))
                    last.then_inc(s_score, 1)
                    pe.wait_ge(s_pick, 1)
                    for k, src in enumerate((place, keep)):
                        for h in range(2):
                            last = nc.tensor.transpose(turn_ps[:, (2 * k + h) * ROWS:(2 * k + h + 1) * ROWS],
                                                       src[:, h * P:(h + 1) * P], ident[0:ROWS, 0:ROWS])
                    last.then_inc(s_turn, 1)

                    def turn(i):
                        wait(pe, s_xtc[i % 2], i // 2)
                        for rr in range(2):
                            for h in range(2):
                                blk = xn[:, (2 * i + rr) * L + h * P:(2 * i + rr) * L + (h + 1) * P]
                                last = nc.tensor.transpose(xt_ps[i % 2][:, (2 * rr + h) * P:(2 * rr + h + 1) * P],
                                                           blk, ident[:, :])
                        last.then_inc(s_xt, 1)

                    turn(0)
                    pe.wait_ge(s_pick, 3)
                    for i in range(ROWS // 2):
                        if i + 1 < ROWS // 2:
                            turn(i + 1)
                        pe.wait_ge(s_xtc[i % 2], i // 2 + 1)
                        for rr in range(2):
                            r = 2 * i + rr
                            q, at = divmod(r, ROWS_PER_BANK)
                            for h in range(2):
                                last = nc.tensor.matmul(pick_ps[q][:, at * TOP:(at + 1) * TOP],
                                                        xt[:, i % 2 * 2 + rr, h, :], picker[:, h, r, :],
                                                        start=(h == 0), stop=(h == 1))
                        last.then_inc(s_feat, 1)

        with Memory(nc, tag + "b") as b_:
            acc = [b_.ps(f"acc{i}", [P, BANK]) for i in range(8)]
            s_bias = sem(f"{tag}_bias_loaded")
            s_h = sem(f"{tag}_hidden_product")
            s_relu = sem(f"{tag}_hidden_ready")
            s_ht = sem(f"{tag}_hidden_turned")
            s_htc = sem(f"{tag}_hidden_turned_copied")
            s_r = sem(f"{tag}_rec_product")
            s_rec = sem(f"{tag}_rec_ready")
            s_grid = sem(f"{tag}_grid_loaded")
            s_o = sem(f"{tag}_out_product")
            s_add = sem(f"{tag}_x_updated")
            banks = lambda width: [(i, min(BANK, width - i * BANK)) for i in range((width + BANK - 1) // BANK)]
            with nc.Block() as block:
                @block.sync
                def _(sp):
                    sp.dma_start(b1, W["b1"].rearrange("(o n) -> o n", o=1)).then_inc(s_bias, 16)
                    sp.dma_start(b2, W["b2"].rearrange("(o n) -> o n", o=1)).then_inc(s_bias, 16)
                    for i in range(WSLOTS, len(tiles)):
                        load_tile(sp, i)
                    sp.wait_ge(s_rec, 7)
                    for o in range(OC):
                        sp.dma_start(xn[o:o + 1, :], rec[:, o * L:(o + 1) * L]).then_inc(s_grid, 16)

                @block.tensor
                def _(pe):
                    def product(w, first, lhs, bias, width):
                        one = C["one"][0:1, 0:ROWS]
                        for i, n in banks(width):
                            nc.tensor.matmul(acc[i][0:ROWS, 0:n], one, bias[:, i * BANK:i * BANK + n],
                                             start=True, stop=False)
                        for k in range(KT):
                            for c in range(2):
                                tile = first + 2 * k + c
                                pe.wait_ge(s_ring[tile % WSLOTS], 16 * (tile // WSLOTS + 1))
                                for i, n in banks(width)[4 * c:4 * c + 4]:
                                    last = nc.tensor.matmul(acc[i][0:ROWS, 0:n], lhs(k),
                                                            ring[:, tile % WSLOTS, (i - 4 * c) * BANK:(i - 4 * c) * BANK + n],
                                                            start=False, stop=(k == KT - 1))
                                last.then_inc(s_used, 1)
                        return last

                    pe.wait_ge(s_bias, 32)
                    product("W1", 0, lambda k: feat[:, k, :], b1, HID)
                    pe.wait_ge(s_relu, 7)
                    for k in range(KT):
                        last = nc.tensor.transpose(acc[k // 8][:, k % 8 * ROWS:(k % 8 + 1) * ROWS],
                                                   hidden[:, k * P:(k + 1) * P], C["ident"][0:ROWS, 0:ROWS])
                        if k % 8 == 7 or k == KT - 1:
                            last.then_inc(s_ht, 1)
                    pe.wait_ge(s_htc, 4)
                    product("W2", 2 * KT, lambda k: hidden_t[:, k, :], b2, OUT)
                    pe.wait_ge(s_grid, 16 * OC)
                    for i in range(ROWS // 2):
                        wait(pe, s_add, i - 7)
                        if i < 8:
                            pe.wait_ge(s_rec, 7)
                        nc.tensor.matmul(acc[i % 8][:, :], out_wt, xn[0:OC, i * BANK:(i + 1) * BANK],
                                         start=True, stop=True).then_inc(s_o, 1)

                @block.scalar
                def _(act):
                    act.wait_ge(s_used, 2 * KT)
                    for i, n in banks(HID):
                        nc.scalar.activation(hidden[:, i * BANK:i * BANK + n], acc[i][0:ROWS, 0:n],
                                             ACT.Relu).then_inc(s_relu, 1)
                    act.wait_ge(s_used, 4 * KT)
                    for i, n in banks(OUT):
                        nc.scalar.activation(rec[:, i * BANK:i * BANK + n], acc[i][0:ROWS, 0:n],
                                             ACT.Copy).then_inc(s_rec, 1)

                @block.vector
                def _(dve):
                    for i in range(4):
                        n = min(8, KT - 8 * i)
                        dve.wait_ge(s_ht, i + 1)
                        nc.vector.tensor_copy(hidden_t[:, 8 * i:8 * i + n, :],
                                              acc[i][:, 0:n * ROWS].rearrange("p (k r) -> p k r", r=ROWS)).then_inc(s_htc, 1)
                    Xv = X[:, :].rearrange("p (n h w) -> p n h w", n=B, h=N)
                    for i in range(ROWS // 2):
                        g, n = divmod(2 * i, B)
                        gi, gj = divmod(g, GRID)
                        dve.wait_ge(s_o, i + 1)
                        for rr in range(2):
                            at = Xv[:, n + rr, gi * SIDE:(gi + 1) * SIDE, gj * SIDE:(gj + 1) * SIDE]
                            last = nc.vector.tensor_tensor(
                                at, at, acc[i % 8][:, rr * L:(rr + 1) * L].rearrange("p (h w) -> p h w", h=SIDE), ALU.add)
                        last.then_inc(s_add, 1)


RING = 4


def attend(nc, sem, tag, X, C, scale_g, bias_g):
    n2, n4 = PIX // 4, PIX // 16
    kept = {2: nc.dram_tensor(f"{tag}_kept2", (P, B * n2), fp32, kind="Internal").ap(),
            4: nc.dram_tensor(f"{tag}_kept4", (P, B * n4), fp32, kind="Internal").ap()}
    with Memory(nc, tag + "p") as pm:
        pooled = {2: pm.sb("pool2", [P, B, n2]), 4: pm.sb("pool4", [P, B, n4])}
        result = {2: pm.sb("out2", [P, B, n2]), 4: pm.sb("out4", [P, B, n4])}
        average(nc, sem, tag, X, pooled, scale_g, bias_g)
        for scale, n in ((4, n4), (2, n2)):
            attention(nc, sem, f"{tag}s{scale}", C, n, pooled[scale], None, result[scale])
        move(nc, sem, tag + "keep", [(kept[k], result[k][:, :, :].rearrange("p b n -> p (b n)")) for k in (2, 4)])
    attention(nc, sem, f"{tag}s1", C, PIX, None, (X, scale_g, bias_g), None)
    with Memory(nc, tag + "q") as pm:
        result = {2: pm.sb("out2", [P, B, n2]), 4: pm.sb("out4", [P, B, n4])}
        move(nc, sem, tag + "back", [(result[k][:, :, :].rearrange("p b n -> p (b n)"), kept[k]) for k in (2, 4)])
        for scale in (2, 4):
            enlarge(nc, sem, f"{tag}e{scale}", X, result[scale], scale)


def move(nc, sem, tag, pairs):
    s = sem(f"{tag}_moved")
    with nc.Block() as block:
        @block.sync
        def _(sp):
            for dst, src in pairs:
                sp.dma_start(dst, src).then_inc(s, 16)
            sp.wait_ge(s, 16 * len(pairs))


def average(nc, sem, tag, X, pooled, scale_g, bias_g):
    with Memory(nc, tag + "v") as m:
        pair = m.sb("pair", [P, N * G])
        quad = m.sb("quad", [P, N // 2 * G])
        four = m.sb("four", [P, N // 2 * G // 2])
        s_step = sem(f"{tag}_average_step")
        with nc.Block() as block:
            @block.vector
            def _(dve):
                n_step = [0]

                def step(ins):
                    n_step[0] += 1
                    ins.then_inc(s_step, 1)
                    dve.wait_ge(s_step, n_step[0])

                for b in range(B):
                    xv = X[:, b * PIX:(b + 1) * PIX].rearrange("p (q e) -> p q e", e=2)
                    rows = pair[:, :].rearrange("p (y e g) -> p y e g", e=2, g=G)
                    qv = quad[:, :].rearrange("p (y g) -> p y g", g=G)
                    out = pooled[2][:, b, :]
                    ov = out.rearrange("p (y g) -> p y g", g=G)
                    per = lambda t: t[:, b * G:(b + 1) * G].unsqueeze(1).to_broadcast([P, N // 2, G])
                    step(nc.vector.tensor_tensor(pair[:, :], xv[:, :, 0], xv[:, :, 1], ALU.add))
                    step(nc.vector.tensor_tensor(qv, rows[:, :, 0, :], rows[:, :, 1, :], ALU.add))
                    step(nc.vector.scalar_tensor_tensor(qv, qv, 0.25, per(scale_g), ALU.mult, ALU.mult))
                    step(nc.vector.tensor_tensor(ov, qv, per(bias_g), ALU.add))
                    o2 = out.rearrange("p (q e) -> p q e", e=2)
                    f = four[:, :].rearrange("p (y e g) -> p y e g", e=2, g=G // 2)
                    o4 = pooled[4][:, b, :].rearrange("p (y g) -> p y g", g=G // 2)
                    step(nc.vector.tensor_tensor(four[:, :], o2[:, :, 0], o2[:, :, 1], ALU.add))
                    step(nc.vector.tensor_tensor(o4, f[:, :, 0, :], f[:, :, 1, :], ALU.add))
                    step(nc.vector.tensor_scalar(o4, o4, 0.25, None, ALU.mult))


def attention(nc, sem, tag, C, n, small, full, small_out):
    W = min(BANK, n)
    NB = n // W
    MT = n // P
    Q = NB * MT
    PER = MT // NB
    ring = min(RING, MT)
    adders = MT > 2
    with Memory(nc, tag) as m:
        if full:
            X, scale_g, bias_g = full
            xn3 = m.sb("xn", [P, 3, n])
        xh = m.sb("xh", [P, 2, n], fp16)
        v = m.sb("v", [P, 2, MT, P])
        e = m.sb("e", [P, ring, W])
        acc = {k: m.sb(f"acc{k}", [P, 2, W]) for k in range(2)}
        tile_max = m.sb("tile_max", [P, Q])
        row_max = m.sb("row_max", [P, MT])
        shift = m.sb("shift", [MT, P], fp16)
        shift_row = m.sb("shift_row", [1, n], fp16)
        ones_row = m.sb("ones_row", [1, P], fp16)
        ones = m.sb("ones", [P, P])
        log_sum = m.sb("log_sum", [P, W])
        inv_sum = m.sb("inv_sum", [P, 2, W])
        out = m.sb("out", [P, 2, W])
        s_ps = [m.ps(f"s_ps{i}", [P, BANK]) for i in range(2)]
        m_ps = [m.ps(f"m_ps{i}", [P, BANK]) for i in range(2)]
        o_ps = [m.ps(f"o_ps{i}", [P, BANK]) for i in range(2)]
        sum_ps = m.ps("sum_ps", [P, BANK])
        t_ps = m.ps("t_ps", [P, BANK])

        s_one = sem(f"{tag}_ones_set")
        s_mul = sem(f"{tag}_x_scaled")
        s_xn = sem(f"{tag}_x_normed")
        s_xh = sem(f"{tag}_x_fp16")
        s_t = sem(f"{tag}_x_turned")
        s_v = sem(f"{tag}_x_turned_copied")
        s_m = sem(f"{tag}_max_scores")
        s_tmax = sem(f"{tag}_tile_max")
        s_rmax = sem(f"{tag}_row_max")
        s_rt = sem(f"{tag}_row_max_turned")
        s_neg = sem(f"{tag}_shift_ready")
        s_row = sem(f"{tag}_shift_row_loaded")
        s_s = sem(f"{tag}_scores")
        s_e = sem(f"{tag}_exp_ready")
        s_pv = sem(f"{tag}_values_added")
        s_add = [sem(f"{tag}_exp_summed_{k}") for k in ("even", "odd")]
        s_sum = sem(f"{tag}_denominator")
        s_log = sem(f"{tag}_denominator_log")
        s_inv = sem(f"{tag}_denominator_inverse")
        s_out = sem(f"{tag}_normalised")
        s_x = sem(f"{tag}_x_updated")

        def x(b):
            return xn3[:, b % 3, :] if full else small[:, b, :]

        ADDS = MT // 2 - 1
        pieces = NB

        def adds_done(block, mt):
            return block * ADDS + max(mt // 2, 1)

        def stage(dve, b, nb):
            cols = bass.ds(nb * W, W)
            if full:
                rows = W // F
                src = X[:, bass.ds(nb * W + b * PIX, W)].rearrange("p (h g e) -> p h g e", h=rows, e=2)
                dst = xn3[:, b % 3, cols].rearrange("p (h g e) -> p h g e", h=rows, e=2)
                per = lambda t: t[:, b * G:(b + 1) * G].unsqueeze(1).unsqueeze(3).to_broadcast([P, rows, G, 2])
                wait(dve, s_pv, (b - 2) * Q)
                wait(dve, s_t, (b - 2) * MT)
                nc.vector.tensor_tensor(dst, src, per(scale_g), ALU.mult).then_inc(s_mul, 1)
                dve.wait_ge(s_mul, b * NB + nb + 1)
                nc.vector.tensor_tensor(dst, dst, per(bias_g), ALU.add).then_inc(s_xn, 1)
                dve.wait_ge(s_xn, b * NB + nb + 1)
            wait(dve, s_m, (b - 1) * Q)
            nc.vector.tensor_copy(xh[:, b % 2, cols], x(b)[:, cols]).then_inc(s_xh, 1)

        def pe_max(pe, b, nb, mt):
            step = b * Q + nb * MT + mt
            if mt == 0:
                wait(pe, s_xh, (b + 1) * pieces)
            wait(pe, s_tmax, step - 1)
            tile = nb * PER + mt // NB
            nc.tensor.matmul(m_ps[mt % 2][:, 0:W], xh[:, b % 2, bass.ds(tile * P, P)],
                             xh[:, b % 2, mt % NB * W:(mt % NB + 1) * W], start=True, stop=True).then_inc(s_m, 1)

        def dve_max(dve, b, nb, mt):
            step = b * Q + nb * MT + mt
            wait(dve, s_m, step + 1)
            wait(dve, s_rmax, b)
            nc.vector.tensor_reduce(tile_max[:, bass.ds(nb * MT + mt, 1)], m_ps[mt % 2][:, 0:W],
                                    axis=AX.X, op=ALU.max).then_inc(s_tmax, 1)

        def pe_close(pe, b):
            for i in range(0, MT, 4):
                bank = s_ps[i // 4 % 2]
                k = min(4, MT - i)
                groups = (MT + 3) // 4
                wait(pe, s_v, b * groups + i // 4 - 1)
                for j in range(k):
                    last = nc.tensor.transpose(bank[:, j * P:(j + 1) * P], x(b)[:, (i + j) * P:(i + j + 1) * P],
                                               C["ident"][:, :])
                last.then_inc(s_t, k)
            wait(pe, s_rmax, b + 1)
            nc.tensor.transpose(t_ps[0:MT, 0:P], row_max[:, :], C["ident"][:, :]).then_inc(s_rt, 1)

        def act_close(act, b):
            for i in range(0, MT, 4):
                k = min(4, MT - i)
                wait(act, s_t, b * MT + i + k)
                nc.scalar.activation(v[:, b % 2, i:i + k, :].rearrange("p a c -> p (a c)"),
                                     s_ps[i // 4 % 2][:, 0:k * P], ACT.Copy).then_inc(s_v, 1)

        def dve_close(dve, b):
            wait(dve, s_tmax, (b + 1) * Q)
            wait(dve, s_rt, b)
            nc.vector.tensor_reduce(row_max[:, :], tile_max[:, :].rearrange("p (t c) -> p t c", c=NB),
                                    axis=AX.X, op=ALU.max).then_inc(s_rmax, 1)
            wait(dve, s_rt, b + 1)
            wait(dve, s_row, 16 * b)
            nc.vector.tensor_scalar(shift[:, :], t_ps[0:MT, 0:P], -1.0, None, ALU.mult).then_inc(s_neg, 1)

        def sp_close(sp, b):
            wait(sp, s_neg, b + 1)
            wait(sp, s_s, b * Q)
            sp.dma_start(shift_row[:, :], shift[:, :]).then_inc(s_row, 16)

        def pe_scores(pe, b, nb, mt):
            step = b * Q + nb * MT + mt
            if mt == 0:
                wait(pe, s_row, 16 * (b + 1))
                wait(pe, s_v, (b + 1) * ((MT + 3) // 4))
            wait(pe, s_e, step - 1)
            cols = bass.ds(nb * W, W)
            nc.tensor.matmul(s_ps[mt % 2][:, 0:W], x(b)[:, mt * P:(mt + 1) * P], x(b)[:, cols], start=True, stop=False)
            nc.tensor.matmul(s_ps[mt % 2][:, 0:W], ones_row[:, :], shift_row[:, cols],
                             start=False, stop=True).then_inc(s_s, 1)

        def pe_values(pe, b, block, par, mt):
            if mt == 0:
                wait(pe, s_out, block - 1)
            wait(pe, s_e, block * MT + mt + 1)
            nc.tensor.matmul(o_ps[par][:, 0:W], v[:, b % 2, mt, :], e[:, mt % ring, :],
                             start=(mt == 0), stop=(mt == MT - 1)).then_inc(s_pv, 1)

        def pe_sum(pe, block, par):
            wait(pe, s_log, block)
            for k in range(2):
                if adders:
                    wait(pe, s_add[k], (block + 1) * ADDS)
                src = acc[k][:, par, :] if adders else e[:, k, :]
                last = nc.tensor.matmul(sum_ps[:, 0:W], ones[:, :], src, start=(k == 0), stop=(k == 1))
            last.then_inc(s_sum, 1)

        def act_exp(act, b, nb, mt):
            step = b * Q + nb * MT + mt
            block = b * NB + nb
            wait(act, s_s, step + 1)
            wait(act, s_pv, step - ring + 1)
            if adders:
                old = (mt - ring) % MT
                wait(act, s_add[mt % 2], adds_done(block if mt >= ring else block - 1, old))
            else:
                wait(act, s_sum, (step - ring) // MT + 1)
            nc.scalar.activation(e[:, mt % ring, :], s_ps[mt % 2][:, 0:W], ACT.Exp).then_inc(s_e, 1)

        def act_inverse(act, block, par):
            wait(act, s_sum, block + 1)
            wait(act, s_inv, block)
            nc.scalar.activation(log_sum[:, :], sum_ps[:, 0:W], ACT.Ln).then_inc(s_log, 1)
            wait(act, s_log, block + 1)
            wait(act, s_out, block - 1)
            nc.scalar.activation(inv_sum[:, par, :], log_sum[:, :], ACT.Exp, scale=-1.0).then_inc(s_inv, 1)

        def add_exp(eng, engine, k, block, par, mt):
            if not adders or mt % 2 != k or mt < 2:
                return
            wait(eng, s_e, block * MT + mt + 1)
            if mt < 4:
                wait(eng, s_sum, block - 1)
                first = e[:, mt - 2, :]
            else:
                wait(eng, s_add[k], block * ADDS + mt // 2 - 1)
                first = acc[k][:, par, :]
            engine.tensor_tensor(acc[k][:, par, :], first, e[:, mt % ring, :], ALU.add).then_inc(s_add[k], 1)

        def dve_out(dve, b, nb, block, par):
            wait(dve, s_inv, block + 1)
            wait(dve, s_pv, (block + 1) * MT)
            if full:
                wait(dve, s_x, block - 1)
                dst = out[:, par, :]
            else:
                dst = small_out[:, b, nb * W:(nb + 1) * W]
            nc.vector.tensor_tensor(dst, inv_sum[:, par, :], o_ps[par][:, 0:W], ALU.mult).then_inc(s_out, 1)

        def pool_out(pool, b, nb, block, par):
            if full:
                wait(pool, s_out, block + 1)
                at = X[:, bass.ds(nb * W + b * PIX, W)]
                nc.gpsimd.tensor_tensor(at, at, out[:, par, :], ALU.add).then_inc(s_x, 1)

        def finish_at(mt):
            return mt == min(3, MT - 1)

        def pe_block(pe, b, nb, par, prev):
            block = b * NB + nb
            for mt in range(MT):
                pe_scores(pe, b, nb, mt)
                if b + 1 < B:
                    pe_max(pe, b + 1, nb, mt)
                if mt:
                    pe_values(pe, b, block, par, mt - 1)
                elif prev:
                    pe_values(pe, b, block - 1, 1 - par, MT - 1)
                if prev and finish_at(mt):
                    pe_sum(pe, block - 1, 1 - par)

        def act_block(act, b, nb, par, prev):
            for mt in range(MT):
                act_exp(act, b, nb, mt)
                if prev and finish_at(mt):
                    act_inverse(act, b * NB + nb - 1, 1 - par)

        def dve_block(dve, b, nb, par, prev):
            block = b * NB + nb
            for mt in range(MT):
                if b + 1 < B:
                    dve_max(dve, b + 1, nb, mt)
                add_exp(dve, nc.vector, 1, block, par, mt)
                if prev and mt == min(4, MT - 1):
                    dve_out(dve, b, nb - 1, block - 1, 1 - par)
            if b + 2 < B:
                stage(dve, b + 2, nb)

        def pool_block(pool, b, nb, par, prev):
            block = b * NB + nb
            for mt in range(MT):
                add_exp(pool, nc.gpsimd, 0, block, par, mt)
                if prev and mt == min(5, MT - 1):
                    pool_out(pool, b, nb - 1, block - 1, 1 - par)

        def blocks(eng, body, b):
            for nb in range(min(2, NB)):
                body(eng, b, nb, nb, nb > 0)
            if NB > 2:
                with eng.Fori(1, NB // 2) as i:
                    body(eng, b, 2 * i, 0, True)
                    body(eng, b, 2 * i + 1, 1, True)

        PAR = (NB - 1) % 2

        with nc.Block() as block_:
            @block_.sync
            def _(sp):
                for b in range(B):
                    sp_close(sp, b)

            @block_.tensor
            def _(pe):
                for nb in range(NB):
                    for mt in range(MT):
                        pe_max(pe, 0, nb, mt)
                pe_close(pe, 0)
                pe.wait_ge(s_one, 2)
                for b in range(B):
                    blocks(pe, pe_block, b)
                    last = (b + 1) * NB - 1
                    pe_values(pe, b, last, PAR, MT - 1)
                    pe_sum(pe, last, PAR)
                    if b + 1 < B:
                        pe_close(pe, b + 1)

            @block_.scalar
            def _(act):
                act.preload_act_table_set(EXP_LN_TABLES)
                act_close(act, 0)
                for b in range(B):
                    blocks(act, act_block, b)
                    act_inverse(act, (b + 1) * NB - 1, PAR)
                    if b + 1 < B:
                        act_close(act, b + 1)

            @block_.vector
            def _(dve):
                nc.vector.memset(ones[:, :], 1.0).then_inc(s_one, 1)
                nc.vector.memset(ones_row[:, :], 1.0).then_inc(s_one, 1)
                for nb in range(NB):
                    stage(dve, 0, nb)
                for nb in range(NB):
                    for mt in range(MT):
                        dve_max(dve, 0, nb, mt)
                for nb in range(NB):
                    stage(dve, 1, nb)
                dve_close(dve, 0)
                for b in range(B):
                    blocks(dve, dve_block, b)
                    dve_out(dve, b, NB - 1, (b + 1) * NB - 1, PAR)
                    if b + 1 < B:
                        dve_close(dve, b + 1)

            @block_.gpsimd
            def _(pool):
                for b in range(B):
                    blocks(pool, pool_block, b)
                    pool_out(pool, b, NB - 1, (b + 1) * NB - 1, PAR)


def enlarge(nc, sem, tag, X, small, scale):
    w = N // scale
    half = scale // 2
    far = [(half - k - 0.5) / scale for k in range(half)]
    with Memory(nc, tag) as m:
        part = m.sb("part", [P, N * w])
        tall = m.sb("tall", [P, N * w])
        wide = m.sb("wide", [P, N * N])
        s_step = sem(f"{tag}_resize_step")
        with nc.Block() as block:
            @block.vector
            def _(dve):
                n_step = [0]

                def done(ins):
                    n_step[0] += 1
                    ins.then_inc(s_step, 1)

                def stretch(src, dst, tmp):
                    for k, weight in enumerate(far):
                        done(nc.vector.tensor_scalar(tmp, src, weight, None, ALU.mult))
                        dve.wait_ge(s_step, n_step[0])
                        for phase, at, by, edge in ((k, slice(1, w), slice(0, w - 1), 0),
                                                    (scale - 1 - k, slice(0, w - 1), slice(1, w), w - 1)):
                            done(nc.vector.scalar_tensor_tensor(dst[:, at, phase, :], src[:, at, :], 1.0 - weight,
                                                                tmp[:, by, :], ALU.mult, ALU.add))
                            done(nc.vector.tensor_copy(dst[:, edge, phase, :], src[:, edge, :]))
                        dve.wait_ge(s_step, n_step[0])

                for b in range(B):
                    src = small[:, b, :].rearrange("p (h w) -> p h w", w=w)
                    stretch(src, tall[:, :].rearrange("p (h s w) -> p h s w", s=scale, w=w),
                            part[:, 0:w * w].rearrange("p (h w) -> p h w", w=w))
                    stretch(tall[:, :].rearrange("p (h w) -> p w h", w=w),
                            wide[:, :].rearrange("p (h w s) -> p w s h", w=w, s=scale),
                            part[:, :].rearrange("p (h w) -> p w h", w=w))
                    xb = X[:, b * PIX:(b + 1) * PIX]
                    done(nc.vector.tensor_tensor(xb, xb, wide[:, :], ALU.add))
                    dve.wait_ge(s_step, n_step[0])


def constants(nc, sem, C):
    s_set = sem("constants_set")
    s_done = sem("constants_done")
    with nc.Block() as block:
        @block.vector
        def _(dve):
            nc.vector.memset(C["mean_of_pairs"][:, :], 1.0 / (2 * P))
            nc.vector.memset(C["mean_of_sums"][:, :], 1.0 / (P * 2 * N))
            nc.vector.memset(C["one"][:, :], 1.0)

        @block.gpsimd
        def _(pool):
            nc.gpsimd.memset(C["ident"][:, :], 0.0).then_inc(s_set, 1)
            nc.gpsimd.memset(C["pick"][:, :], 0.0).then_inc(s_set, 1)
            pool.wait_ge(s_set, 2)
            nc.gpsimd.affine_select(out=C["ident"][:, :], in_=C["ident"][:, :], compare_op=ALU.not_equal, fill=1.0,
                                    base=0, pattern=[[-1, P]], channel_multiplier=1).then_inc(s_done, 1)
            rows = C["pick"][:, :].rearrange("k (s m) -> k s m", m=P)
            for part in range(3):
                if part:
                    pool.wait_ge(s_done, part + 1)
                nc.gpsimd.affine_select(out=rows, in_=rows, compare_op=ALU.not_equal, fill=1.0,
                                        base=-2 * S * part, pattern=[[-1, 2 * S], [0, P]],
                                        channel_multiplier=1).then_inc(s_done, 1)


def load_x(nc, sem, x, X):
    s = sem("x_loaded")
    with nc.Block() as block:
        @block.sync
        def _(sp):
            for b in range(B):
                sp.dma_start(X[:, b * PIX:(b + 1) * PIX], x[b].rearrange("t n f -> t (n f)")).then_inc(s, 16)
            sp.wait_ge(s, B * 16)


def store_x(nc, sem, X, out):
    s = sem("x_stored")
    with nc.Block() as block:
        @block.sync
        def _(sp):
            for b in range(B):
                sp.dma_start(out[b].rearrange("t n f -> t (n f)"), X[:, b * PIX:(b + 1) * PIX]).then_inc(s, 16)
            sp.wait_ge(s, B * 16)


def program(nc, ins, out):
    stack = ExitStack()
    with stack:
        def sem(name):
            return stack.enter_context(nc.semaphore(name))

        def sb(name, shape, dt=fp32):
            return stack.enter_context(nc.sbuf_tensor(name, shape, dt))

        X = sb("X", [P, B * PIX])
        C = {"ident": sb("ident", [P, P]), "mean_of_pairs": sb("mean_of_pairs", [P, P]),
             "mean_of_sums": sb("mean_of_sums", [P, P]), "one": sb("one", [P, P])}
        scale_g = sb("scale_g", [P, B * G])
        bias_g = sb("bias_g", [P, B * G])
        with Memory(nc, "mamba") as m:
            C["pick"] = m.sb("pick", [3 * 2 * S, 2 * S * P], bf16)
            constants(nc, sem, C)
            load_x(nc, sem, ins["x"], X)
            for layer in range(2):
                tag = f"l{layer}"
                with Memory(nc, tag + "m") as lm, Semaphores(nc) as sem_l:
                    M = {"taps": lm.sb("taps", [P, (TAPS + 1) * D]), "w_dt": lm.sb("w_dt", [P, D]),
                         "w_bc": lm.sb("w_bc", [P, 3 * 2 * S]), "w_out": lm.sb("w_out", [P, F]),
                         "diag_Dp": lm.sb("diag_Dp", [P, D]), "A": lm.sb("A", [P, S]),
                         "conv_b": lm.sb("conv_b", [P, 1]), "neg_conv_b": lm.sb("neg_conv_b", [P, 1]),
                         "b_dt": lm.sb("b_dt", [P, 1])}
                    scale_c = lm.sb("scale_c", [P, CHUNKS])
                    bias_c = lm.sb("bias_c", [P, CHUNKS])
                    W = {k: ins[f"L{layer}_conv_{k}"] for k in
                         ("W_in", "conv_w", "conv_b", "W_x", "W_dt", "b_dt", "A_log", "Dp", "W_out")}
                    mamba_weights(nc, sem_l, tag, W, C, M)
                    group_norm_stats(nc, sem_l, tag + "g", X, C, scale_g, bias_g)
                    mamba_norm(nc, sem_l, tag, scale_g, bias_g, C, scale_c, bias_c)
                    mamba_layer(nc, sem_l, tag, X, C, M, scale_c, bias_c)
        group_norm_stats(nc, sem, "l2g", X, C, scale_g, bias_g)
        top_blocks(nc, sem, "l2", X, C, {k: ins[f"L2_conv_{k}"] for k in
                   ("conv_w", "W1", "b1", "W2", "b2", "out_w")}, scale_g, bias_g)
        group_norm_stats(nc, sem, "l3g", X, C, scale_g, bias_g)
        attend(nc, sem, "l3", X, C, scale_g, bias_g)
        store_x(nc, sem, X, out)


def kernel(**inputs):
    import numpy as np
    import concourse.bacc as bacc
    from concourse.bass_utils import run_bass_kernel_spmd

    nc = bacc.Bacc("TRN2", target_bir_lowering=False, num_devices=1)
    arrays, ins = {}, {}
    for name, a in inputs.items():
        a = np.ascontiguousarray(a)
        arrays[f"in_{name}"] = a
        ins[name] = nc.dram_tensor(f"in_{name}", a.shape, mybir.dt.from_np(a.dtype), kind="ExternalInput").ap()
    out = nc.dram_tensor("out", (B, T, N, F), fp32, kind="ExternalOutput").ap()
    program(nc, ins, out)
    return run_bass_kernel_spmd(nc, [arrays], core_ids=[0]).results[0]["out"]
```
